# Optimizing a Trainium2 kernel written in Bass

```python
import numpy as np
import jax
import jax.numpy as jnp

def _softmax(x, axis=-1):
    return jax.nn.softmax(x, axis=axis)

def _gelu(x):
    return jax.nn.gelu(x, approximate=True)

def _silu(x):
    return jax.nn.silu(x)

def _sigmoid(x):
    return jax.nn.sigmoid(x)

def _layernorm(x, axis=-1, eps=1e-05):
    m = jnp.mean(x, axis=axis, keepdims=True)
    v = jnp.var(x, axis=axis, keepdims=True)
    return (x - m) / jnp.sqrt(v + eps)

def _scatter_add(tgt, idx, src, axis=0):
    return tgt.at[idx].add(src)

def _segment_sum(src, seg, n):
    return jax.ops.segment_sum(src, seg, n)
kernel_name = 'mk_macaron_d1_jaxref_r8_24705e'

def setup_inputs(seed: int=0):
    np.random.seed(seed)
    _w = jnp.asarray

    def _L0_attn_setup():
        import jax, jax.numpy as jnp
        import numpy as np
        D_MODEL = 128
        D_INNER = 256
        D_STATE = 16
        DT_RANK = 64
        D_CONV = 4
        EPS = 1e-05
        B_SZ, L = (2, 256)

        def _silu(x):
            return x * jax.nn.sigmoid(x)
        key = jax.random.key(seed)
        ks = jax.random.split(key, 8)
        s = 0.02
        inp = {'x': jax.random.normal(ks[0], (B_SZ, L, D_MODEL), jnp.float32), 'in_proj_w': jax.random.normal(ks[1], (D_MODEL, 2 * D_INNER), jnp.float32) * s, 'conv_w': jax.random.normal(ks[2], (D_INNER, 1, D_CONV), jnp.float32) * s, 'conv_b': jnp.zeros((D_INNER,), jnp.float32), 'x_proj_w': jax.random.normal(ks[3], (D_INNER, DT_RANK + 2 * D_STATE), jnp.float32) * s, 'dt_proj_w': jax.random.normal(ks[4], (DT_RANK, D_INNER), jnp.float32) * s, 'dt_proj_b': jax.random.normal(ks[5], (D_INNER,), jnp.float32) * s, 'A_log': jnp.log(jnp.broadcast_to(jnp.arange(1, D_STATE + 1, dtype=jnp.float32), (D_INNER, D_STATE))), 'D': jnp.ones((D_INNER,), jnp.float32), 'out_proj_w': jax.random.normal(ks[6], (D_INNER, D_MODEL), jnp.float32) * s, 'norm_w': jnp.ones((D_MODEL,), jnp.float32)}
        return inp
    _L0_attn_in = _L0_attn_setup()

    def _L0_ffn_setup():
        import jax, jax.numpy as jnp
        import numpy as np
        TOP_K = 2
        key = jax.random.key(seed)
        k0, k1, k2, k3 = jax.random.split(key, 4)
        B, T, C, E, F = (4, 256, 128, 8, 512)
        x = jax.random.normal(k0, (B, T, C), dtype=jnp.float32)
        gate_w = jax.random.normal(k1, (C, E), dtype=jnp.float32) * 0.02
        w1 = jax.random.normal(k2, (E, C, F), dtype=jnp.float32) * 0.02
        w2 = jax.random.normal(k3, (E, F, C), dtype=jnp.float32) * 0.02
        return {'x': x, 'gate_w': gate_w, 'w1': w1, 'w2': w2}
    _L0_ffn_in = _L0_ffn_setup()
    _d = {'L0_attn_x': _L0_attn_in['x'], 'L0_attn_in_proj_w': _L0_attn_in['in_proj_w'], 'L0_attn_conv_w': _L0_attn_in['conv_w'], 'L0_attn_conv_b': _L0_attn_in['conv_b'], 'L0_attn_x_proj_w': _L0_attn_in['x_proj_w'], 'L0_attn_dt_proj_w': _L0_attn_in['dt_proj_w'], 'L0_attn_dt_proj_b': _L0_attn_in['dt_proj_b'], 'L0_attn_A_log': _L0_attn_in['A_log'], 'L0_attn_D': _L0_attn_in['D'], 'L0_attn_out_proj_w': _L0_attn_in['out_proj_w'], 'L0_attn_norm_w': _L0_attn_in['norm_w'], 'L0_ffn_gate_w': _L0_ffn_in['gate_w'], 'L0_ffn_w1': _L0_ffn_in['w1'], 'L0_ffn_w2': _L0_ffn_in['w2']}
    _x0 = _d['L0_attn_x']
    _d['L0_attn_x'] = jax.random.normal(jax.random.fold_in(jax.random.key(seed), 1), (16, 256, 128), dtype=_x0.dtype)
    del _x0
    return _d

def reference(L0_attn_x, L0_attn_in_proj_w, L0_attn_conv_w, L0_attn_conv_b, L0_attn_x_proj_w, L0_attn_dt_proj_w, L0_attn_dt_proj_b, L0_attn_A_log, L0_attn_D, L0_attn_out_proj_w, L0_attn_norm_w, L0_ffn_gate_w, L0_ffn_w1, L0_ffn_w2):

    def _L0_attn_ref(x, in_proj_w, conv_w, conv_b, x_proj_w, dt_proj_w, dt_proj_b, A_log, D, out_proj_w, norm_w):
        import jax, jax.numpy as jnp
        import numpy as np
        D_MODEL = 128
        D_INNER = 256
        D_STATE = 16
        DT_RANK = 64
        D_CONV = 4
        EPS = 1e-05
        B_SZ, L = (2, 256)

        def _silu(x):
            return x * jax.nn.sigmoid(x)
        b, l, d = x.shape
        xn = x * jax.lax.rsqrt(jnp.mean(x * x, axis=-1, keepdims=True) + EPS) * norm_w
        x_and_res = xn @ in_proj_w
        xi, res = jnp.split(x_and_res, 2, axis=-1)
        xc = jax.lax.conv_general_dilated(xi.transpose(0, 2, 1), conv_w, window_strides=(1,), padding=[(D_CONV - 1, 0)], feature_group_count=D_INNER, dimension_numbers=('NCH', 'OIH', 'NCH')) + conv_b[None, :, None]
        xi = _silu(xc.transpose(0, 2, 1))
        x_dbl = xi @ x_proj_w
        delta, Bm, Cm = jnp.split(x_dbl, [DT_RANK, DT_RANK + D_STATE], axis=-1)
        delta = jax.nn.softplus(delta @ dt_proj_w + dt_proj_b)
        A = -jnp.exp(A_log)
        deltaA = jnp.exp(delta[..., None] * A)
        deltaB_u = delta[..., None] * Bm[:, :, None, :] * xi[..., None]

        def step(state, inputs):
            dA_t, dBu_t, C_t = inputs
            state = dA_t * state + dBu_t
            y_t = jnp.einsum('bdn,bn->bd', state, C_t)
            return (state, y_t)
        state0 = jnp.zeros((b, D_INNER, D_STATE), xi.dtype)
        _, ys = jax.lax.scan(step, state0, (deltaA.transpose(1, 0, 2, 3), deltaB_u.transpose(1, 0, 2, 3), Cm.transpose(1, 0, 2)))
        y = ys.transpose(1, 0, 2) + xi * D
        y = y * _silu(res)
        out = y @ out_proj_w + x
        return out

    def _L0_ffn_ref(x, gate_w, w1, w2):
        import jax, jax.numpy as jnp
        import numpy as np
        TOP_K = 2
        E = gate_w.shape[-1]
        probs = jax.nn.softmax(x @ gate_w, axis=-1)
        topw, topi = jax.lax.top_k(probs, TOP_K)
        topw = topw / topw.sum(axis=-1, keepdims=True)
        combine = (jax.nn.one_hot(topi, E, dtype=x.dtype) * topw[..., None]).sum(axis=-2)

        def body(acc, params):
            w1_i, w2_i, cw = params
            h = jax.nn.gelu(x @ w1_i, approximate=False)
            return (acc + cw[..., None] * (h @ w2_i), None)
        acc0 = jnp.zeros_like(x)
        out, _ = jax.lax.scan(body, acc0, (w1, w2, jnp.moveaxis(combine, -1, 0)))
        return out
    x = L0_attn_x
    x = x + 0.5 * _L0_ffn_ref(_layernorm(x, axis=-1), L0_ffn_gate_w, L0_ffn_w1, L0_ffn_w2)
    x = x + _L0_attn_ref(_layernorm(x, axis=-1), L0_attn_in_proj_w, L0_attn_conv_w, L0_attn_conv_b, L0_attn_x_proj_w, L0_attn_dt_proj_w, L0_attn_dt_proj_b, L0_attn_A_log, L0_attn_D, L0_attn_out_proj_w, L0_attn_norm_w)
    x = x + 0.5 * _L0_ffn_ref(_layernorm(x, axis=-1), L0_ffn_gate_w, L0_ffn_w1, L0_ffn_w2)
    return x

_drawn_inputs = setup_inputs


def setup_inputs(seed=0):
    import zlib

    import numpy as np

    out = dict(_drawn_inputs(seed))
    spreads = {'L0_attn_conv_b': (0.0, 0.8), 'L0_attn_D': (1.0, 0.6), 'L0_attn_norm_w': (1.0, 0.6)}
    factors = {'L0_attn_in_proj_w': 8.0,
     'L0_attn_conv_w': 8.0,
     'L0_attn_x_proj_w': 8.0,
     'L0_attn_dt_proj_w': 8.0,
     'L0_attn_dt_proj_b': 8.0,
     'L0_attn_A_log': 8.0,
     'L0_attn_out_proj_w': 8.0}
    for name, (base, spread) in spreads.items():
        noise = np.random.default_rng([zlib.crc32(name.encode()), seed]).standard_normal(out[name].shape)
        drawn = base * np.exp(spread * noise) if base else spread * noise
        out[name] = jnp.asarray(drawn.astype(out[name].dtype))
    for name, factor in factors.items():
        out[name] = (out[name] * factor).astype(out[name].dtype)
    return out
```

```python
import concourse.bass as bass
from concourse import mybir
from contextlib import ExitStack

F32 = mybir.dt.float32
F32R = mybir.dt.float32r
BF16 = mybir.dt.bfloat16
I32 = mybir.dt.int32
U32 = mybir.dt.uint32
ALU = mybir.AluOpType
ACT = mybir.ActivationFunctionType

P = 128
BATCH, SEQ, C = 16, 256, 128
E, F = 8, 512
DI, NST, RANK, TAPS = 256, 16, 64, 4
W_CHUNK = 2
EPS = 1e-5
RSQRT_GUESS = float(0x5F3759DF)

TILES = BATCH * SEQ // P
PAIR_TILES = 4
PAIRS = TILES // PAIR_TILES
SEQ_TILES = SEQ // P
TOK = PAIR_TILES * P
KF = F // P
HALVES = DI // P
XP = RANK + 2 * NST
BC = 2 * NST
UNITS = NST // 2
UNIT = 2 * HALVES * SEQ

FIRST_FULL, END_FULL, LAST = 2, PAIRS - 1, PAIRS + 1

SEQ_START = (1, 15)
TRANSPOSE, CONV, GATE, XPROJ, DTPROJ = range(5)
UNIT0 = 6
SCAN_LAG, SUM_LAG = 1, 3
YFIN = UNIT0 + UNITS + SUM_LAG
OUTP = YFIN + 1
SEQ_END = OUTP + 1
FRONT_PLACES = (TRANSPOSE, CONV, GATE, XPROJ, DTPROJ, *range(UNIT0, UNIT0 + UNITS), OUTP)


class Stages:

    def __init__(self, j, ffn1, ssm, ffn2, next_route):
        self.j, self.ffn1, self.ssm, self.ffn2 = j, ffn1, ssm, ffn2
        order = sorted([(e, 0, e) for e in range(E) if ffn1] + [(e + 1.5, 1, e) for e in range(E) if ffn2])
        self.steps = [(s, e) for _, s, e in order]
        lead = 0 if ffn1 else 2
        self.l1 = {2 * (i + lead): i for i in range(len(self.steps))}
        self.l2 = {slot + 3: i for slot, i in self.l1.items()}
        self.combine = {slot + 4: i for slot, i in self.l1.items()}
        self.routes = [(0, 2, 1, -2)] if ffn2 else []
        self.seq_norm = None
        if ffn1:
            last = [slot for slot, i in self.l1.items() if self.steps[i][0] == 0][-1]
            self.seq_norm = last + 5
            if next_route:
                self.routes.append((last + 2, last + 3, 0, 1))
        ends = [max(self.combine) + 1] + ([SEQ_START[1] + SEQ_END + 1] if ssm else [])
        self.slots = max(ends + [r[1] + 3 for r in self.routes] + [self.seq_norm + 1 if ffn1 else 0])
        full = not isinstance(j, int)
        self.ffn_before = 16 * j - 16 if full or j > 0 and j < LAST and j != 1 else {0: 0, 1: 8, LAST: 16 * PAIRS - 8}[j]
        self.routes_before = 2 * j - 1 if full or 0 < j < PAIRS and j != 1 else {0: 1, 1: 2, PAIRS: 14, LAST: 15}[j]
        self.seqs_before = 2 * j - 2 if full or j else 0
        self.front_before = 2 * self.routes_before + len(FRONT_PLACES) * self.seqs_before
        order = []
        for slot in range(self.slots):
            for r, (_, at, _, _) in enumerate(self.routes):
                if slot == at:
                    order.append(("rows", r))
                if slot == at + 1:
                    order.append(("logits", r))
            order += [(at, q) for q, at in self.seq_tasks(slot) if at in FRONT_PLACES]
        self.front_at = {use: n for n, use in enumerate(order)}

    def seq_tasks(self, slot):
        if not self.ssm:
            return []
        return [(q, slot - SEQ_START[q]) for q in range(2) if 0 <= slot - SEQ_START[q] <= SEQ_END]

    def front(self, *use):
        return self.front_before + self.front_at[use]

    def pair(self, stage):
        return self.j - (2 if stage else 0)


def some(count):
    return not isinstance(count, int) or count > 0


def macaron_mamba_moe(nc, x, in_proj_w, conv_w, conv_b, x_proj_w, dt_proj_w, dt_proj_b, A_log, D,
                      out_proj_w, norm_w, gate_w, w1, w2, out):
    ctx = ExitStack()
    with ctx:
        def sb(name, shape, dt=F32):
            return ctx.enter_context(nc.sbuf_tensor(name, shape, dt))

        def ps(name, shape):
            return ctx.enter_context(nc.psum_tensor(name, shape, F32))

        def sem(name):
            return ctx.enter_context(nc.semaphore(name))

        x_rows = x.rearrange("b (s p) c -> p (b s) c", p=P)
        out_rows = out.rearrange("b (s p) c -> p (b s) c", p=P)

        x_all = sb("x_all", [P, TILES, C])
        w1_hi = sb("w1_hi", [P, E, F], F32R)
        w1_lo = sb("w1_lo", [P, E, F], F32R)
        w2_sb = sb("w2_sb", [P, E, KF, C])
        gate_sb = sb("gate_sb", [P, E])
        inproj_sb = sb("inproj_sb", [P, 2 * DI])
        taps_sb = sb("taps_sb", [P, DI, TAPS])
        normw_sb = sb("normw_sb", [P, 1])
        convw_sb = sb("convw_sb", [P, TAPS, DI])
        resw_sb = sb("resw_sb", [P, DI])
        convb_sb = sb("convb_sb", [P, HALVES])
        dtb_sb = sb("dtb_sb", [P, HALVES])
        d_sb = sb("d_sb", [P, HALVES])
        alog_sb = sb("alog_sb", [P, HALVES, NST])
        a_sb = sb("a_sb", [P, HALVES, NST])
        xproj_sb = sb("xproj_sb", [P, HALVES, XP])
        xbc_sb = sb("xbc_sb", [P, HALVES, 3, BC])
        dtproj_sb = sb("dtproj_sb", [RANK, DI])
        outproj_sb = sb("outproj_sb", [P, HALVES, C])
        ident = sb("ident", [P, P])
        pick = sb("pick", [3 * BC, BC, P], BF16)
        expert_ids = sb("expert_ids", [P, E])
        route_rows = sb("route_rows", [P, PAIR_TILES, C])
        seq_rows = sb("seq_rows", [P, PAIR_TILES, C])
        stats = sb("stats", [P, PAIR_TILES, 6])
        moments = sb("moments", [P, PAIR_TILES, 2])
        rs_in = sb("rs_in", [P, PAIR_TILES])
        rs_half = sb("rs_half", [P, PAIR_TILES])
        rs_int = sb("rs_int", [P, PAIR_TILES], I32)
        rs_t = sb("rs_t", [P, PAIR_TILES])
        rstd = sb("rstd", [P, PAIR_TILES])
        rstd2 = sb("rstd2", [P, PAIR_TILES])
        rms_in = sb("rms_in", [P, PAIR_TILES])
        lnT = sb("lnT", [P, TOK])
        lnT_hi = [sb(f"lnT_hi{s}", [P, TOK], F32R) for s in range(2)]
        lnT_lo = [sb(f"lnT_lo{s}", [P, TOK], F32R) for s in range(2)]
        combine_w = [sb(f"combine_w{s}", [P, PAIR_TILES, E]) for s in range(2)]
        logits = sb("logits", [P, PAIR_TILES, E])
        top = sb("top", [P, PAIR_TILES, 8])
        top_at = sb("top_at", [P, PAIR_TILES, 8], U32)
        top_atf = sb("top_atf", [P, PAIR_TILES, 2])
        top_gap = sb("top_gap", [P, PAIR_TILES])
        top_exp = sb("top_exp", [P, PAIR_TILES])
        top_sum = sb("top_sum", [P, PAIR_TILES])
        top_w = sb("top_w", [P, PAIR_TILES, 2])
        onehot = sb("onehot", [P, 2, PAIR_TILES, E])
        hT = sb("hT", [P, 2, KF, TOK])
        xnT = sb("xnT", [P, TAPS - 1 + SEQ])
        lrow = sb("lrow", [P, PAIR_TILES, C])
        xi = sb("xi", [P, 2, HALVES, SEQ])
        sres = sb("sres", [P, 2, HALVES, SEQ])
        rank_sb = sb("rank_sb", [RANK, SEQ])
        bc_f = sb("bc_f", [3 * BC, SEQ])
        bc_mid = sb("bc_mid", [3 * BC, SEQ], BF16)
        bc3 = sb("bc3", [3 * BC, SEQ], BF16)
        z = sb("z", [P, HALVES, SEQ])
        zneg = sb("zneg", [P, HALVES, SEQ])
        ez = sb("ez", [P, HALVES, SEQ])
        ez1 = sb("ez1", [P, HALVES, SEQ])
        lnz = sb("lnz", [P, HALVES, SEQ])
        delta = sb("delta", [P, HALVES, SEQ])
        udx = sb("udx", [P, HALVES, SEQ])
        NDA = 4
        dA = sb("dA", [P, NDA, 2, HALVES, SEQ])
        w1_sb = dA[:, :, :, :, :].rearrange("p u n h t -> p (u n h t)").rearrange("p (e f) -> p e f", e=E)
        NDBU = 3
        dBu = sb("dBu", [P, NDBU, 2, HALVES, SEQ])
        state = sb("state", [P, 2, 2, HALVES, SEQ])
        cs = sb("cs", [P, 2, 2, SEQ])
        prod = sb("prod", [P, 2, 2, HALVES, SEQ])
        yskip = sb("yskip", [P, HALVES, SEQ])
        yT = sb("yT", [P, HALVES, SEQ])

        hP = ps("hP", [P, 2, 2, TOK])
        oP = ps("oP", [P, PAIR_TILES, C])
        front = ps("front", [P, TOK])
        bP = ps("bP", [P, 2, SEQ])
        yP = ps("yP", [P, HALVES, SEQ])

        x0_in = sem("x0_in")
        x_in = sem("x_in")
        gate_in = sem("gate_in")
        w1_in = [sem(f"w1_in{c}") for c in range(E // W_CHUNK)]
        w2_in = [sem(f"w2_in{c}") for c in range(E // W_CHUNK)]
        w1_split = sem("w1_split")
        small_in = sem("small_in")
        ident_ready = sem("ident_ready")
        ident_zero = sem("ident_zero")
        a_exp_ready = sem("a_exp_ready")
        a_ready = sem("a_ready")
        ssm_weights_ready = sem("ssm_weights_ready")
        route_rows_ready = sem("route_rows_ready")
        seq_rows_ready = sem("seq_rows_ready")
        lnT_ready = sem("lnT_ready")
        front_full = sem("front_full")
        front_read = sem("front_read")
        gap_ready = sem("gap_ready")
        gap_exp_ready = sem("gap_exp_ready")
        h_full = sem("h_full")
        gelu_done = sem("gelu_done")
        o_full = sem("o_full")
        combined = sem("combined")
        sp_arg = sem("sp_arg")
        sp_act = sem("sp_act")
        delta_ready = sem("delta_ready")
        dA_ready = sem("dA_ready")
        bc3_ready = sem("bc3_ready")
        b_full = sem("b_full")
        b_read = sem("b_read")
        scan_done = sem("scan_done")
        prod_ready = sem("prod_ready")
        prod_done = sem("prod_done")
        sum_done = sem("sum_done")
        y_ready = sem("y_ready")
        out_done = sem("out_done")

        block = ctx.enter_context(nc.Block())
        SMALL_DMAS = 11

        def iterations(eng, body):
            body(Stages(0, True, False, False, True))
            body(Stages(1, True, True, False, True))
            with eng.Fori(FIRST_FULL, END_FULL) as j:
                body(Stages(j, True, True, True, True))
            body(Stages(PAIRS - 1, True, True, True, False))
            body(Stages(PAIRS, False, True, True, False))
            body(Stages(LAST, False, False, True, False))

        @block.sync
        def _(sp):
            sp.dma_start(x_all[:, 0:PAIR_TILES, :], x_rows[:, 0:PAIR_TILES, :]).then_inc(x0_in, 16)
            sp.dma_start(gate_sb[:, :], gate_w).then_inc(gate_in, 16)
            for c in range(E // W_CHUNK):
                es = slice(c * W_CHUNK, (c + 1) * W_CHUNK)
                sp.dma_start(w1_sb[:, es, :], w1[es].rearrange("e c f -> c e f")).then_inc(w1_in[c], 16)
                sp.dma_start(w2_sb[:, es, :, :], w2[es].rearrange("e (k p) c -> p e k c", p=P)).then_inc(w2_in[c], 16)
            sp.dma_start(x_all[:, PAIR_TILES:, :], x_rows[:, PAIR_TILES:, :]).then_inc(x_in, 16)

            def body(st):
                if st.ffn2:
                    sp.wait_ge(combined, st.ffn_before + len(st.steps))
                    t = st.pair(1) * PAIR_TILES
                    sp.dma_start(out_rows[:, bass.ds(t, PAIR_TILES), :],
                                 x_all[:, bass.ds(t, PAIR_TILES), :]).then_inc(out_done, 16)
            iterations(sp, body)
            sp.wait_ge(out_done, 16 * PAIRS)

        @block.gpsimd
        def _(pool):
            pool.memset(ident[:, :], 0.0).then_inc(ident_zero, 1)
            pool.wait_ge(ident_zero, 1)
            pool.affine_select(out=ident[:, :], in_=ident[:, :], compare_op=ALU.not_equal, fill=1.0,
                               base=0, pattern=[[-1, P]], channel_multiplier=1).then_inc(ident_ready, 1)
            pool.iota(expert_ids[:, :], [[1, E]], base=0, channel_multiplier=0,
                      allow_small_or_imprecise_dtypes=True).then_inc(ident_ready, 1)

            def body(st):
                for slot in range(st.slots):
                    for q, at in st.seq_tasks(slot):
                        if UNIT0 <= at - SCAN_LAG < UNIT0 + UNITS:
                            k = at - SCAN_LAG - UNIT0
                            u = (st.seqs_before + q) * UNITS + k
                            pool.wait_ge(scan_done, u + 1)
                            pool.wait_ge(front_read, st.front(UNIT0 + k, q) + 1)
                            if some(u - 1):
                                pool.wait_ge(sum_done, u - 1)
                            pool.tensor_tensor(prod[:, k % 2], state[:, k % 2],
                                               cs[:, k % 2].unsqueeze(2).broadcast_to([P, 2, HALVES, SEQ]),
                                               ALU.mult).then_inc(prod_ready, 1)
                            pool.wait_ge(prod_ready, u + 1)
                            pool.tensor_tensor(prod[:, k % 2, 0], prod[:, k % 2, 0], prod[:, k % 2, 1],
                                               ALU.add).then_inc(prod_done, 1)
            iterations(pool, body)

        @block.scalar
        def _(act):
            act.dma_start(inproj_sb[:, :], in_proj_w).then_inc(small_in, 16)
            act.dma_start(taps_sb[:, :, :], conv_w.rearrange("d o k -> (o d) k").partition_broadcast(P)).then_inc(small_in, 16)
            act.dma_start(normw_sb[:, :], norm_w.rearrange("(p o) -> p o", o=1)).then_inc(small_in, 16)
            with nc.allow_non_contiguous_dma(reason="vectors of 256 over partitions"):
                act.dma_start(convb_sb[:, :], conv_b.rearrange("(h p) -> p h", p=P)).then_inc(small_in, 16)
                act.dma_start(dtb_sb[:, :], dt_proj_b.rearrange("(h p) -> p h", p=P)).then_inc(small_in, 16)
                act.dma_start(d_sb[:, :], D.rearrange("(h p) -> p h", p=P)).then_inc(small_in, 16)
            act.dma_start(alog_sb[:, :, :], A_log.rearrange("(h p) n -> p h n", p=P)).then_inc(small_in, 16)
            act.dma_start(xproj_sb[:, :, :], x_proj_w.rearrange("(h p) n -> p h n", p=P)).then_inc(small_in, 16)
            act.dma_start(dtproj_sb[:, :], dt_proj_w).then_inc(small_in, 16)
            act.dma_start(outproj_sb[:, :, :], out_proj_w.rearrange("(h p) n -> p h n", p=P)).then_inc(small_in, 16)
            act.dma_start(xbc_sb[:, :, 0, :], x_proj_w[:, RANK:XP].rearrange("(h p) n -> p h n", p=P)).then_inc(small_in, 16)
            act.wait_ge(small_in, 16 * SMALL_DMAS)
            act.preload_act_table_set("natural_log_exp_and_others")
            act.activation(a_sb[:, :, :], alog_sb[:, :, :], ACT.Exp).then_inc(a_exp_ready, 1)

            def router_exp(r):
                act.preload_act_table_set("natural_log_exp_and_others")
                act.wait_ge(gap_ready, r + 1)
                act.activation(top_exp[:, :], top_gap[:, :], ACT.Exp).then_inc(gap_exp_ready, 1)

            def body(st):
                if isinstance(st.j, int) and st.j == 1:
                    act.wait_ge(a_ready, 1)
                for slot in range(st.slots):
                    if slot in st.l1:
                        i = st.l1[slot]
                        f = st.ffn_before + i
                        act.preload_act_table_set("gelu_and_others")
                        if some(f - 1):
                            act.wait_ge(o_full, f - 1)
                        for g in range(2):
                            act.wait_ge(h_full, 2 * f + g + 1)
                            act.activation(hT[:, i % 2, 2 * g:2 * g + 2, :], hP[:, g], ACT.Gelu).then_inc(gelu_done, 1)
                    for r, (_, at, _, _) in enumerate(st.routes):
                        if slot == at + 2:
                            router_exp(st.routes_before + r)
                    for q, at in st.seq_tasks(slot):
                        m = st.seqs_before + q
                        if at == CONV:
                            act.preload_act_table_set("silu_and_others")
                            act.wait_ge(front_full, st.front(at, q) + 1)
                            if some(m - 1):
                                act.wait_ge(y_ready, m - 1)
                            for h in range(HALVES):
                                ins = act.activation(xi[:, q, h, :], front[:, h * SEQ:(h + 1) * SEQ], ACT.Silu,
                                                     bias=convb_sb[:, h:h + 1])
                            ins.then_inc(front_read, 1)
                        if at == GATE:
                            act.preload_act_table_set("silu_and_others")
                            act.wait_ge(front_full, st.front(at, q) + 1)
                            act.activation(sres[:, q, :, :], front[:, :].rearrange("p (h t) -> p h t", h=HALVES),
                                           ACT.Silu).then_inc(front_read, 1)
                        if at == DTPROJ + 1:
                            act.preload_act_table_set("natural_log_exp_and_others")
                            act.wait_ge(sp_arg, 2 * m + 1)
                            act.activation(ez[:, :, :], zneg[:, :, :], ACT.Exp).then_inc(sp_act, 1)
                            act.wait_ge(sp_arg, 2 * m + 2)
                            act.activation(lnz[:, :, :], ez1[:, :, :], ACT.Ln).then_inc(sp_act, 1)
                        if UNIT0 <= at < UNIT0 + UNITS:
                            k = at - UNIT0
                            if k % 2 == 0:
                                act.preload_act_table_set("natural_log_exp_and_others")
                                if k == 0:
                                    act.wait_ge(delta_ready, m + 1)
                                for kk in (k, k + 1):
                                    u = m * UNITS + kk
                                    if some(u - NDA + 1):
                                        act.wait_ge(scan_done, u - NDA + 1)
                                    for n in range(2):
                                        for h in range(HALVES):
                                            ins = act.activation(dA[:, kk % NDA, n, h, 1:SEQ], delta[:, h, 1:SEQ], ACT.Exp,
                                                                 scale=a_sb[:, h, 2 * kk + n:2 * kk + n + 1])
                                    ins.then_inc(dA_ready, 1)
                            u = m * UNITS + k
                            act.wait_ge(front_full, st.front(at, q) + 1)
                            if some(u - 1):
                                act.wait_ge(prod_done, u - 1)
                            act.activation(cs[:, k % 2], front[:, :].rearrange("p (n t) -> p n t", n=2),
                                           ACT.Copy).then_inc(front_read, 1)
            router_exp(0)
            iterations(act, body)

        @block.vector
        def _(dve):
            def rsqrt(dst, src, eps):
                n = slice(0, src.shape[1])
                dve.tensor_scalar(rs_in[:, n], src, eps, None, ALU.add)
                dve.drain()
                dve.tensor_scalar(rs_int[:, n], rs_in[:, n].bitcast(I32), 1, None, ALU.logical_shift_right)
                dve.tensor_scalar(rs_half[:, n], rs_in[:, n], -0.5, None, ALU.mult)
                dve.drain()
                dve.tensor_scalar(dst.bitcast(I32), rs_int[:, n], -1.0, RSQRT_GUESS, ALU.mult, ALU.add)
                dve.drain()
                for _ in range(3):
                    dve.tensor_tensor(rs_t[:, n], dst, dst, ALU.mult)
                    dve.drain()
                    dve.tensor_tensor(rs_t[:, n], rs_t[:, n], rs_half[:, n], ALU.mult)
                    dve.drain()
                    dve.scalar_tensor_tensor(dst, rs_t[:, n], 1.5, dst, ALU.add, ALU.mult)
                    dve.drain()

            def mean_and_var(t0, n):
                dve.drain()
                for i in range(n):
                    dve.bn_stats(stats[:, i, :], x_all[:, bass.ds(t0 + i, 1), :].squeeze(1))
                dve.drain()
                for i in range(n):
                    dve.bn_aggr(moments[:, i, :], stats[:, i, :])
                dve.drain()

            def normalise(t0):
                mean_and_var(t0, PAIR_TILES)
                rsqrt(rstd[:, :], moments[:, :, 1], EPS)
                for i in range(PAIR_TILES):
                    ins = dve.tensor_scalar(route_rows[:, i, :], x_all[:, bass.ds(t0 + i, 1), :].squeeze(1),
                                            moments[:, i, 0:1], rstd[:, i:i + 1], ALU.subtract, ALU.mult)
                ins.then_inc(route_rows_ready, 1)

            def normalise_seqs(t0):
                xs = x_all[:, bass.ds(t0, PAIR_TILES), :]
                mean_and_var(t0, PAIR_TILES)
                rsqrt(rstd[:, :], moments[:, :, 1], EPS)
                dve.tensor_tensor(rms_in[:, :], rstd[:, :], rstd[:, :], ALU.mult)
                for i in range(PAIR_TILES):
                    dve.tensor_scalar(lrow[:, i, :], x_all[:, bass.ds(t0 + i, 1), :].squeeze(1),
                                      moments[:, i, 0:1], rstd[:, i:i + 1], ALU.subtract, ALU.mult)
                dve.drain()
                dve.tensor_tensor(rms_in[:, :], rms_in[:, :], moments[:, :, 1], ALU.mult)
                dve.tensor_tensor(xs, xs, lrow[:, :, :], ALU.add)
                dve.drain()
                rsqrt(rstd2[:, :], rms_in[:, :], EPS)
                for i in range(PAIR_TILES):
                    ins = dve.tensor_scalar(seq_rows[:, i, :], lrow[:, i, :], rstd2[:, i:i + 1], None, ALU.mult)
                ins.then_inc(seq_rows_ready, 1)

            def take_rows(s, use):
                dve.wait_ge(front_full, use + 1)
                dve.tensor_copy(lnT_hi[s][:, :], front[:, :])
                dve.tensor_copy(lnT[:, :], front[:, :]).then_inc(front_read, 1)
                dve.drain()
                dve.tensor_tensor(lnT_lo[s][:, :], lnT[:, :], lnT_hi[s][:, :].bitcast(F32), ALU.subtract).then_inc(lnT_ready, 1)

            def route(s, r, use):
                dve.wait_ge(front_full, use + 1)
                dve.tensor_copy(logits[:, :, :].rearrange("p t e -> p (t e)"),
                                front[:, 0:PAIR_TILES * E]).then_inc(front_read, 1)
                dve.drain()
                for i in range(PAIR_TILES):
                    dve.max(top[:, i, :], logits[:, i, :])
                dve.drain()
                dve.tensor_tensor(top_gap[:, :], top[:, :, 1], top[:, :, 0], ALU.subtract).then_inc(gap_ready, 1)
                for i in range(PAIR_TILES):
                    dve.max_index(top_at[:, i, :], top[:, i, :], logits[:, i, :])
                dve.drain()
                dve.tensor_copy(top_atf[:, :, :], top_at[:, :, 0:2])
                dve.wait_ge(gap_exp_ready, r + 1)
                dve.tensor_scalar(top_sum[:, :], top_exp[:, :], 1.0, None, ALU.add)
                dve.drain()
                dve.reciprocal(top_sum[:, :], top_sum[:, :])
                dve.drain()
                dve.tensor_scalar(top_w[:, :, 0], top_sum[:, :], 0.5, None, ALU.mult)
                dve.scalar_tensor_tensor(top_w[:, :, 1], top_exp[:, :], 0.5, top_sum[:, :], ALU.mult, ALU.mult)
                full = [P, PAIR_TILES, E]
                for k in range(2):
                    dve.tensor_tensor(onehot[:, k], expert_ids[:, :].unsqueeze(1).broadcast_to(full),
                                      top_atf[:, :, k:k + 1].broadcast_to(full), ALU.is_equal)
                dve.drain()
                for k in range(2):
                    dve.tensor_tensor(onehot[:, k], onehot[:, k], top_w[:, :, k:k + 1].broadcast_to(full), ALU.mult)
                dve.drain()
                dve.tensor_tensor(combine_w[s][:, :, :], onehot[:, 0], onehot[:, 1], ALU.add)
                dve.drain()

            def split_w1(c):
                es = slice(c * W_CHUNK, (c + 1) * W_CHUNK)
                dve.wait_ge(w1_in[c], 16)
                dve.tensor_copy(w1_hi[:, es, :], w1_sb[:, es, :])
                dve.drain()
                dve.tensor_tensor(w1_lo[:, es, :], w1_sb[:, es, :], w1_hi[:, es, :].bitcast(F32),
                                  ALU.subtract).then_inc(w1_split, 1)

            dve.wait_ge(x0_in, 16)
            normalise(0)
            take_rows(0, 0)
            split_w1(0)
            dve.wait_ge(ident_ready, 2)
            route(0, 0, 1)
            for c in range(1, E // W_CHUNK):
                split_w1(c)
            dve.drain()

            def ssm_weights():
                dve.wait_ge(small_in, 16 * SMALL_DMAS)
                dve.tensor_scalar(inproj_sb[:, :], inproj_sb[:, :], normw_sb[:, 0:1], None, ALU.mult)
                dve.memset(xnT[:, 0:TAPS - 1], 0.0)
                dve.memset(dA[:, :, :, :, 0:1], 0.0)
                dve.drain()
                for k in range(TAPS):
                    dve.tensor_tensor(convw_sb[:, k, :], inproj_sb[:, 0:DI], taps_sb[:, :, k], ALU.mult)
                dve.tensor_copy(resw_sb[:, :], inproj_sb[:, DI:])
                for part in (1, 2):
                    dve.tensor_copy(xbc_sb[:, :, part, :], xbc_sb[:, :, 0, :])
                dve.wait_ge(ident_ready, 2)
                for part in range(3):
                    r = slice(part * BC, (part + 1) * BC)
                    dve.tensor_copy(pick[r], ident[r, r].unsqueeze(2).broadcast_to([BC, BC, P]))
                dve.drain()
                dve.wait_ge(a_exp_ready, 1)
                dve.tensor_scalar(a_sb[:, :, :], a_sb[:, :, :], -1.0, None, ALU.mult).then_inc(a_ready, 1)


            def body(st):
                if isinstance(st.j, int) and st.j == 0:
                    dve.wait_ge(x_in, 16)
                for slot in range(st.slots):
                    if slot in st.combine:
                        i = st.combine[slot]
                        s, e = st.steps[i]
                        t0 = st.pair(s) * PAIR_TILES
                        dve.wait_ge(o_full, st.ffn_before + i + 1)
                        if some(st.ffn_before + i):
                            dve.wait_ge(combined, st.ffn_before + i)
                        for t in range(PAIR_TILES):
                            xt = x_all[:, bass.ds(t0 + t, 1), :].squeeze(1)
                            ins = dve.scalar_tensor_tensor(xt, oP[:, t, :], combine_w[s][:, t, e:e + 1], xt,
                                                           ALU.mult, ALU.add)
                        ins.then_inc(combined, 1)
                    for r, (norm, at, s, ahead) in enumerate(st.routes):
                        if slot == norm:
                            normalise((st.j + ahead) * PAIR_TILES)
                        if slot == at + 1:
                            take_rows(s, st.front("rows", r))
                        if slot == at + 2:
                            route(s, st.routes_before + r, st.front("logits", r))
                    if slot == st.seq_norm:
                        normalise_seqs(st.j * PAIR_TILES)
                    for q, at in st.seq_tasks(slot):
                        m = st.seqs_before + q
                        t0 = (st.j - 1) * PAIR_TILES + q * SEQ_TILES
                        xs = x_all[:, bass.ds(t0, SEQ_TILES), :]
                        if at == TRANSPOSE + 1:
                            dve.wait_ge(front_full, st.front(TRANSPOSE, q) + 1)
                            dve.tensor_copy(xnT[:, TAPS - 1:], front[:, 0:SEQ]).then_inc(front_read, 1)
                        if at == XPROJ + 1:
                            dve.wait_ge(front_full, st.front(XPROJ, q) + 1)
                            dve.tensor_copy(rank_sb[:, :], front[0:RANK, 0:SEQ])
                            dve.tensor_copy(bc_f[:, :], front[0:3 * BC, SEQ:2 * SEQ])
                            dve.tensor_copy(bc3[:, :], front[0:3 * BC, SEQ:2 * SEQ]).then_inc(front_read, 1)
                            dve.drain()
                            dve.tensor_tensor(bc_f[:, :], bc_f[:, :], bc3[:, :], ALU.subtract)
                            dve.drain()
                            dve.tensor_copy(bc_mid[:, :], bc_f[:, :])
                            dve.drain()
                            dve.tensor_copy(bc3[BC:2 * BC, :], bc_mid[BC:2 * BC, :])
                            dve.tensor_tensor(bc3[2 * BC:3 * BC, :], bc_f[2 * BC:3 * BC, :], bc_mid[2 * BC:3 * BC, :],
                                              ALU.subtract)
                            dve.drain()
                            dve.sem_inc(bc3_ready, 1)
                        if at == DTPROJ + 1:
                            dve.wait_ge(front_full, st.front(DTPROJ, q) + 1)
                            for h in range(HALVES):
                                ins = dve.tensor_scalar(z[:, h, :], front[:, h * SEQ:(h + 1) * SEQ],
                                                        dtb_sb[:, h:h + 1], None, ALU.add)
                            ins.then_inc(front_read, 1)
                            dve.drain()
                            dve.scalar_tensor_tensor(zneg[:, :, :], z[:, :, :], -1.0, z[:, :, :], ALU.mult,
                                                     ALU.min).then_inc(sp_arg, 1)
                            dve.wait_ge(sp_act, 2 * m + 1)
                            dve.tensor_scalar(ez1[:, :, :], ez[:, :, :], 1.0, None, ALU.add).then_inc(sp_arg, 1)
                            dve.drain()
                            dve.scalar_tensor_tensor(ez[:, :, :], ez1[:, :, :], -1.0, ez[:, :, :], ALU.add, ALU.subtract)
                            dve.drain()
                            dve.wait_ge(sp_act, 2 * m + 2)
                            dve.tensor_tensor(lnz[:, :, :], lnz[:, :, :], ez[:, :, :], ALU.subtract)
                            dve.drain()
                            if some(m):
                                dve.wait_ge(dA_ready, m * UNITS)
                            dve.scalar_tensor_tensor(delta[:, :, :], z[:, :, :], 0.0, lnz[:, :, :], ALU.max,
                                                     ALU.add).then_inc(delta_ready, 1)
                            dve.drain()
                            dve.tensor_tensor(udx[:, :, :], delta[:, :, :], xi[:, q, :, :], ALU.mult)
                            dve.drain()
                        if UNIT0 <= at < UNIT0 + UNITS:
                            k = at - UNIT0
                            shape = [P, 2, HALVES, SEQ]
                            u = m * UNITS + k
                            dve.wait_ge(b_full, u + 1)
                            if some(u - NDBU + 1):
                                dve.wait_ge(scan_done, u - NDBU + 1)
                            dve.tensor_tensor(dBu[:, k % NDBU], udx[:, :, :].unsqueeze(1).broadcast_to(shape),
                                              bP[:, :, :].unsqueeze(2).broadcast_to(shape), ALU.mult).then_inc(b_read, 1)
                        if UNIT0 <= at - SCAN_LAG < UNIT0 + UNITS:
                            k = at - SCAN_LAG - UNIT0
                            u = m * UNITS + k
                            dve.wait_ge(b_read, u + 1)
                            dve.wait_ge(dA_ready, u + 1)
                            if some(u - 1):
                                dve.wait_ge(prod_done, u - 1)
                            dve.tensor_tensor_scan(state[:, k % 2].rearrange("p n h t -> p (n h t)"),
                                                   dA[:, k % NDA].rearrange("p n h t -> p (n h t)"),
                                                   dBu[:, k % NDBU].rearrange("p n h t -> p (n h t)"),
                                                   0.0, ALU.mult, ALU.add).then_inc(scan_done, 1)
                        if at == YFIN:
                            dve.wait_ge(sum_done, (m + 1) * UNITS)
                            for h in range(HALVES):
                                dve.scalar_tensor_tensor(yskip[:, h, :], xi[:, q, h, :], d_sb[:, h:h + 1], yP[:, h, :],
                                                         ALU.mult, ALU.add)
                            dve.drain()
                            dve.tensor_tensor(yT[:, :, :], yskip[:, :, :], sres[:, q], ALU.mult).then_inc(y_ready, 1)
                        if at == OUTP + 1:
                            dve.wait_ge(front_full, st.front(OUTP, q) + 1)
                            dve.tensor_tensor(xs, xs, front[:, 0:SEQ_TILES * C].rearrange("p (t c) -> p t c", c=C),
                                              ALU.add).then_inc(front_read, 1)
                            dve.drain()
            ssm_weights()
            dve.sem_inc(ssm_weights_ready, 1)
            iterations(dve, body)

        @block.tensor
        def _(pe):
            pe.wait_ge(ident_ready, 2)

            def transpose_rows(r, use):
                pe.wait_ge(route_rows_ready, r + 1)
                if some(use):
                    pe.wait_ge(front_read, use)
                for t in range(PAIR_TILES):
                    ins = pe.transpose(front[:, t * P:(t + 1) * P], route_rows[:, t, :], ident[:, :])
                ins.then_inc(front_full, 1)

            def router_logits(r, use):
                pe.wait_ge(front_read, use)
                pe.wait_ge(lnT_ready, r + 1)
                for t in range(PAIR_TILES):
                    ins = pe.matmul(front[:, t * E:(t + 1) * E], lnT[:, t * P:(t + 1) * P], gate_sb[:, :],
                                    start=True, stop=True)
                ins.then_inc(front_full, 1)

            transpose_rows(0, 0)
            pe.wait_ge(gate_in, 16)
            router_logits(0, 1)

            def body(st):
                if isinstance(st.j, int) and st.j == 1:
                    pe.wait_ge(ssm_weights_ready, 1)
                for slot in range(st.slots):
                    if slot in st.l1:
                        i = st.l1[slot]
                        s, e = st.steps[i]
                        f = st.ffn_before + i
                        first_use = isinstance(st.j, int) and st.j == 0
                        if first_use and e % W_CHUNK == 0:
                            pe.wait_ge(w1_split, e // W_CHUNK + 1)
                        for g in range(2):
                            if some(2 * f + g - 1):
                                pe.wait_ge(gelu_done, 2 * f + g - 1)
                            for k in range(2):
                                c0 = (2 * g + k) * P
                                pe.matmul(hP[:, g, k, :], w1_hi[:, e, c0:c0 + P], lnT_hi[s][:, :], start=True, stop=False)
                                pe.matmul(hP[:, g, k, :], w1_hi[:, e, c0:c0 + P], lnT_lo[s][:, :], start=False, stop=False)
                                ins = pe.matmul(hP[:, g, k, :], w1_lo[:, e, c0:c0 + P], lnT_hi[s][:, :], start=False, stop=True)
                            ins.then_inc(h_full, 1)
                    if slot in st.l2:
                        i = st.l2[slot]
                        s, e = st.steps[i]
                        f = st.ffn_before + i
                        if isinstance(st.j, int) and st.j == 0 and e % W_CHUNK == 0:
                            pe.wait_ge(w2_in[e // W_CHUNK], 16)
                        pe.wait_ge(gelu_done, 2 * f + 2)
                        if some(f):
                            pe.wait_ge(combined, f)
                        for t in range(PAIR_TILES):
                            for k in range(KF):
                                ins = pe.matmul(oP[:, t, :], hT[:, i % 2, k, t * P:(t + 1) * P], w2_sb[:, e, k, :],
                                                start=k == 0, stop=k == KF - 1)
                        ins.then_inc(o_full, 1)
                    for r, (_, at, _, _) in enumerate(st.routes):
                        if slot == at:
                            transpose_rows(st.routes_before + r, st.front("rows", r))
                        if slot == at + 1:
                            router_logits(st.routes_before + r, st.front("logits", r))
                    for q, at in st.seq_tasks(slot):
                        m = st.seqs_before + q
                        if at in FRONT_PLACES:
                            before = st.front(at, q)
                            if at >= UNIT0 and at < UNIT0 + UNITS:
                                u = m * UNITS + at - UNIT0
                                if at == UNIT0:
                                    pe.wait_ge(bc3_ready, m + 1)
                                if some(u):
                                    pe.wait_ge(b_read, u)
                                for n in range(2):
                                    ins = pe.matmul(bP[:, n, :], pick[:, 2 * (at - UNIT0) + n, :], bc3[:, :],
                                                    start=True, stop=True)
                                ins.then_inc(b_full, 1)
                            if some(before):
                                pe.wait_ge(front_read, before)
                            if at == TRANSPOSE:
                                pe.wait_ge(seq_rows_ready, st.j)
                                for t in range(SEQ_TILES):
                                    ins = pe.transpose(front[:, t * P:(t + 1) * P], seq_rows[:, q * SEQ_TILES + t, :], ident[:, :])
                            elif at == CONV:
                                for h in range(HALVES):
                                    for k in range(TAPS):
                                        ins = pe.matmul(front[:, h * SEQ:(h + 1) * SEQ], convw_sb[:, k, h * P:(h + 1) * P],
                                                        xnT[:, k:k + SEQ], start=k == 0, stop=k == TAPS - 1)
                            elif at == GATE:
                                for h in range(HALVES):
                                    ins = pe.matmul(front[:, h * SEQ:(h + 1) * SEQ], resw_sb[:, h * P:(h + 1) * P],
                                                    xnT[:, TAPS - 1:], start=True, stop=True)
                            elif at == XPROJ:
                                for h in range(HALVES):
                                    ins = pe.matmul(front[0:RANK, 0:SEQ], xproj_sb[:, h, 0:RANK], xi[:, q, h, :],
                                                    start=h == 0, stop=h == HALVES - 1)
                                for h in range(HALVES):
                                    ins = pe.matmul(front[0:3 * BC, SEQ:2 * SEQ],
                                                    xbc_sb[:, h].rearrange("p r n -> p (r n)"), xi[:, q, h, :],
                                                    start=h == 0, stop=h == HALVES - 1)
                            elif at == DTPROJ:
                                for h in range(HALVES):
                                    ins = pe.matmul(front[:, h * SEQ:(h + 1) * SEQ], dtproj_sb[:, h * P:(h + 1) * P],
                                                    rank_sb[:, :], start=True, stop=True)
                            elif at == OUTP:
                                pe.wait_ge(y_ready, m + 1)
                                for t in range(SEQ_TILES):
                                    for h in range(HALVES):
                                        ins = pe.matmul(front[:, t * C:(t + 1) * C], yT[:, h, t * P:(t + 1) * P],
                                                        outproj_sb[:, h, :], start=h == 0, stop=h == HALVES - 1)
                            else:
                                for n in range(2):
                                    ins = pe.matmul(front[:, n * SEQ:(n + 1) * SEQ], pick[:, NST + 2 * (at - UNIT0) + n, :],
                                                    bc3[:, :], start=True, stop=True)
                            ins.then_inc(front_full, 1)
                        k = at - UNIT0 - SUM_LAG
                        if 0 <= k < UNITS:
                            u = m * UNITS + k
                            if k == 0 and some(m):
                                pe.wait_ge(y_ready, m)
                            pe.wait_ge(prod_done, u + 1)
                            ins = pe.matmul(yP[:, :, :].rearrange("p h t -> p (h t)"), ident[:, :],
                                            prod[:, k % 2, 0].rearrange("p h t -> p (h t)"),
                                            start=k == 0, stop=k == UNITS - 1)
                            ins.then_inc(sum_done, 1)
            iterations(pe, body)


_INS = ["L0_attn_x", "L0_attn_in_proj_w", "L0_attn_conv_w", "L0_attn_conv_b", "L0_attn_x_proj_w",
        "L0_attn_dt_proj_w", "L0_attn_dt_proj_b", "L0_attn_A_log", "L0_attn_D", "L0_attn_out_proj_w",
        "L0_attn_norm_w", "L0_ffn_gate_w", "L0_ffn_w1", "L0_ffn_w2"]


def kernel(**inputs):
    import numpy as _np
    import concourse.bacc as _bacc
    from concourse import mybir as _mybir
    from concourse.bass_utils import run_bass_kernel_spmd as _run

    nc = _bacc.Bacc("TRN2", target_bir_lowering=False, num_devices=1)
    arrays, args = {}, []
    for name in _INS:
        a = _np.ascontiguousarray(inputs[name])
        arrays[f"in_{name}"] = a
        args.append(nc.dram_tensor(f"in_{name}", a.shape, _mybir.dt.from_np(a.dtype), kind="ExternalInput").ap())
    out = nc.dram_tensor("out", (BATCH, SEQ, C), F32, kind="ExternalOutput").ap()
    macaron_mamba_moe(nc, *args, out)
    r = _run(nc, [arrays], core_ids=[0])
    return r.results[0]["out"]
```

```python
import concourse.bass as bass
from concourse import mybir
from contextlib import ExitStack

F32 = mybir.dt.float32
F32R = mybir.dt.float32r
BF16 = mybir.dt.bfloat16
I32 = mybir.dt.int32
U32 = mybir.dt.uint32
ALU = mybir.AluOpType
ACT = mybir.ActivationFunctionType

P = 128
BATCH, SEQ, C = 16, 256, 128
E, F = 8, 512
DI, NST, RANK, TAPS = 256, 16, 64, 4
W_CHUNK = 2
EPS = 1e-5
RSQRT_GUESS = float(0x5F3759DF)

TILES = BATCH * SEQ // P
PAIR_TILES = 4
PAIRS = TILES // PAIR_TILES
SEQ_TILES = SEQ // P
TOK = PAIR_TILES * P
KF = F // P
HALVES = DI // P
XP = RANK + 2 * NST
BC = 2 * NST
UNITS = NST // 2
UNIT = 2 * HALVES * SEQ

FIRST_FULL, END_FULL, LAST = 2, PAIRS - 1, PAIRS + 1

SEQ_START = (0, 13)
SEQ_START_ONE_FFN = (1, 11)
TRANSPOSE, CONV, XPROJ, DTPROJ = 0, 1, 3, 4
UNIT_PLACES = tuple(6 + 3 * (k // 2) + k % 2 for k in range(UNITS))
UNIT_PLACES_ONE_FFN = tuple(6 + k for k in range(UNITS))
SCAN_LAG, SUM_LAG = 1, 3
FRONT_USES = 4 + UNITS + 1
B_USES = 1 + UNITS


class Stages:

    def __init__(self, j, ffn1, ssm, ffn2, next_route):
        self.j, self.ffn1, self.ssm, self.ffn2 = j, ffn1, ssm, ffn2
        self.seq_start = SEQ_START if ffn1 and ffn2 else SEQ_START_ONE_FFN
        self.unit_places = UNIT_PLACES if ffn1 and ffn2 else UNIT_PLACES_ONE_FFN
        self.yfin = self.unit_places[-1] + SUM_LAG + 1
        self.outp = self.yfin + 1
        self.front_places = (TRANSPOSE, CONV, XPROJ, DTPROJ, *self.unit_places, self.outp)
        self.seq_end = self.outp + 1
        order = sorted([(e, 0, e) for e in range(E) if ffn1] + [(e + 3.5, 1, e) for e in range(E) if ffn2])
        self.steps = [(s, e) for _, s, e in order]
        lead = 0 if ffn1 else 1
        self.l1 = {2 * (i + lead): i for i in range(len(self.steps))}
        self.l2 = {slot + 3: i for slot, i in self.l1.items()}
        self.combine = {slot + 4: i for slot, i in self.l1.items()}
        self.routes = [(1, 5, 11, 1, -2) if ffn1 else (0, 0, 4, 1, -2)] if ffn2 else []
        self.seq_norm = None
        if ffn1:
            last = [slot for slot, i in self.l1.items() if self.steps[i][0] == 0][-1]
            self.seq_norm = last + 5
            if next_route:
                self.routes.append((last - 5, last + 2 if ffn2 else last + 3, last + 7, 0, 1))
        ends = [max(self.combine) + 1] + ([self.seq_start[1] + self.seq_end + 1] if ssm else [])
        self.slots = max(ends + [r[2] + 2 for r in self.routes] + [self.seq_norm + 1 if ffn1 else 0])
        full = not isinstance(j, int)
        self.ffn_before = 16 * j - 16 if full or j > 0 and j < LAST and j != 1 else {0: 0, 1: 8, LAST: 16 * PAIRS - 8}[j]
        self.routes_before = 2 * j - 1 if full or 0 < j < PAIRS and j != 1 else {0: 1, 1: 2, PAIRS: 14, LAST: 15}[j]
        self.seqs_before = 2 * j - 2 if full or j else 0
        self.front_before = 2 * self.routes_before + FRONT_USES * self.seqs_before
        order = []
        for slot in range(self.slots):
            order += [("rows", r) for r, route in enumerate(self.routes) if slot == route[1]]
            order += [(at, q) for q, at in self.seq_tasks(slot) if at in self.front_places]
            order += [("logits", r) for r, route in enumerate(self.routes) if slot == route[1] + 3]
        self.front_at = {use: n for n, use in enumerate(order)}
        order = [(at, q) for slot in range(self.slots) for q, at in self.seq_tasks(slot)
                 if at == CONV or self.unit(at) is not None]
        self.b_before = B_USES * self.seqs_before
        self.b_at = {use: n for n, use in enumerate(order)}

    def seq_tasks(self, slot):
        if not self.ssm:
            return []
        return [(q, slot - self.seq_start[q]) for q in range(2) if 0 <= slot - self.seq_start[q] <= self.seq_end]

    def unit(self, place):
        return self.unit_places.index(place) if place in self.unit_places else None

    def front(self, *use):
        return self.front_before + self.front_at[use]

    def b_bank(self, *use):
        return self.b_before + self.b_at[use]

    def pair(self, stage):
        return self.j - (2 if stage else 0)


def some(count):
    return not isinstance(count, int) or count > 0


def macaron_mamba_moe(nc, x, in_proj_w, conv_w, conv_b, x_proj_w, dt_proj_w, dt_proj_b, A_log, D,
                      out_proj_w, norm_w, gate_w, w1, w2, out):
    ctx = ExitStack()
    with ctx:
        def sb(name, shape, dt=F32):
            return ctx.enter_context(nc.sbuf_tensor(name, shape, dt))

        def ps(name, shape):
            return ctx.enter_context(nc.psum_tensor(name, shape, F32))

        def sem(name):
            return ctx.enter_context(nc.semaphore(name))

        x_rows = x.rearrange("b (s p) c -> p (b s) c", p=P)
        out_rows = out.rearrange("b (s p) c -> p (b s) c", p=P)

        x_all = sb("x_all", [P, TILES, C])
        w1_hi = sb("w1_hi", [P, E, F], F32R)
        w1_lo = sb("w1_lo", [P, E, F], F32R)
        w2_sb = sb("w2_sb", [P, E, KF, C])
        gate_sb = sb("gate_sb", [P, E])
        inproj_sb = sb("inproj_sb", [P, 2 * DI])
        taps_sb = sb("taps_sb", [P, DI, TAPS])
        normw_sb = sb("normw_sb", [P, 1])
        convw_sb = sb("convw_sb", [P, TAPS, DI])
        resw_sb = sb("resw_sb", [P, DI])
        convb_sb = sb("convb_sb", [P, HALVES])
        dtb_sb = sb("dtb_sb", [P, HALVES])
        d_sb = sb("d_sb", [P, HALVES])
        alog_sb = sb("alog_sb", [P, HALVES, NST])
        a_sb = sb("a_sb", [P, HALVES, NST])
        xproj_sb = sb("xproj_sb", [P, HALVES, XP])
        xbc_sb = sb("xbc_sb", [P, HALVES, 3, BC])
        dtproj_sb = sb("dtproj_sb", [RANK, DI])
        outproj_sb = sb("outproj_sb", [P, HALVES, C])
        ident = sb("ident", [P, P])
        pick = sb("pick", [3 * BC, BC, P], BF16)
        expert_ids = sb("expert_ids", [P, E])
        route_rows = sb("route_rows", [P, PAIR_TILES, C])
        seq_rows = sb("seq_rows", [P, PAIR_TILES, C])
        stats = sb("stats", [P, PAIR_TILES, 6])
        moments = sb("moments", [P, PAIR_TILES, 2])
        rs_in = sb("rs_in", [P, PAIR_TILES])
        rs_half = sb("rs_half", [P, PAIR_TILES])
        rs_int = sb("rs_int", [P, PAIR_TILES], I32)
        rs_t = sb("rs_t", [P, PAIR_TILES])
        rstd = sb("rstd", [P, PAIR_TILES])
        rstd2 = sb("rstd2", [P, PAIR_TILES])
        rms_in = sb("rms_in", [P, PAIR_TILES])
        lnT = sb("lnT", [P, TOK])
        lnT_hi = [sb(f"lnT_hi{s}", [P, TOK], F32R) for s in range(2)]
        lnT_lo = [sb(f"lnT_lo{s}", [P, TOK], F32R) for s in range(2)]
        combine_w = [sb(f"combine_w{s}", [P, PAIR_TILES, E]) for s in range(2)]
        logits = sb("logits", [P, PAIR_TILES, E])
        top = sb("top", [P, PAIR_TILES, 8])
        top_at = sb("top_at", [P, PAIR_TILES, 8], U32)
        top_atf = sb("top_atf", [P, PAIR_TILES, 2])
        top_gap = sb("top_gap", [P, PAIR_TILES])
        top_exp = sb("top_exp", [P, PAIR_TILES])
        top_sum = sb("top_sum", [P, PAIR_TILES])
        top_w = sb("top_w", [P, PAIR_TILES, 2])
        onehot = sb("onehot", [P, 2, PAIR_TILES, E])
        hT = sb("hT", [P, 2, KF, TOK])
        xnT = sb("xnT", [P, TAPS - 1 + SEQ])
        lrow = sb("lrow", [P, PAIR_TILES, C])
        xi = sb("xi", [P, 2, HALVES, SEQ])
        sres = sb("sres", [P, 2, HALVES, SEQ])
        rank_sb = sb("rank_sb", [RANK, SEQ])
        bc_f = sb("bc_f", [3 * BC, SEQ])
        bc_mid = sb("bc_mid", [3 * BC, SEQ], BF16)
        bc3 = sb("bc3", [3 * BC, SEQ], BF16)
        z = sb("z", [P, HALVES, SEQ])
        zneg = sb("zneg", [P, HALVES, SEQ])
        ez = sb("ez", [P, HALVES, SEQ])
        ez1 = sb("ez1", [P, HALVES, SEQ])
        lnz = sb("lnz", [P, HALVES, SEQ])
        delta = sb("delta", [P, HALVES, SEQ])
        udx = sb("udx", [P, HALVES, SEQ])
        NDA = 4
        dA = sb("dA", [P, NDA, 2, HALVES, SEQ])
        w1_sb = dA[:, :, :, :, :].rearrange("p u n h t -> p (u n h t)").rearrange("p (e f) -> p e f", e=E)
        NDBU = 3
        dBu = sb("dBu", [P, NDBU, 2, HALVES, SEQ])
        state = sb("state", [P, 2, 2, HALVES, SEQ])
        cs = sb("cs", [P, 2, 2, SEQ])
        prod = sb("prod", [P, 2, 2, HALVES, SEQ])
        ysum = sb("ysum", [P, HALVES, SEQ])
        yT = sb("yT", [P, HALVES, SEQ])

        hP = ps("hP", [P, 2, 2, TOK])
        oP = ps("oP", [P, 2, PAIR_TILES, C])
        front = ps("front", [P, TOK])
        bP = ps("bP", [P, 2, SEQ])

        x0_in = sem("x0_in")
        x_in = sem("x_in")
        gate_in = sem("gate_in")
        w1_in = [sem(f"w1_in{c}") for c in range(E // W_CHUNK)]
        w2_in = [sem(f"w2_in{c}") for c in range(E // W_CHUNK)]
        w1_split = sem("w1_split")
        small_in = sem("small_in")
        ident_ready = sem("ident_ready")
        ident_zero = sem("ident_zero")
        a_exp_ready = sem("a_exp_ready")
        a_ready = sem("a_ready")
        ssm_weights_ready = sem("ssm_weights_ready")
        route_rows_ready = sem("route_rows_ready")
        seq_rows_ready = sem("seq_rows_ready")
        lnT_ready = sem("lnT_ready")
        front_full = sem("front_full")
        front_read = sem("front_read")
        gap_ready = sem("gap_ready")
        gap_exp_ready = sem("gap_exp_ready")
        h_full = sem("h_full")
        gelu_done = sem("gelu_done")
        o_full = sem("o_full")
        combined = sem("combined")
        sp_arg = sem("sp_arg")
        sp_act = sem("sp_act")
        delta_ready = sem("delta_ready")
        dA_ready = sem("dA_ready")
        bc3_ready = sem("bc3_ready")
        b_full = sem("b_full")
        b_read = sem("b_read")
        scan_done = sem("scan_done")
        prod_ready = sem("prod_ready")
        prod_added = sem("prod_added")
        sum_done = sem("sum_done")
        y_ready = sem("y_ready")
        out_done = sem("out_done")

        block = ctx.enter_context(nc.Block())
        SMALL_DMAS = 11

        def iterations(eng, body):
            body(Stages(0, True, False, False, True))
            body(Stages(1, True, True, False, True))
            with eng.Fori(FIRST_FULL, END_FULL) as j:
                body(Stages(j, True, True, True, True))
            body(Stages(PAIRS - 1, True, True, True, False))
            body(Stages(PAIRS, False, True, True, False))
            body(Stages(LAST, False, False, True, False))

        @block.sync
        def _(sp):
            sp.dma_start(x_all[:, 0:PAIR_TILES, :], x_rows[:, 0:PAIR_TILES, :]).then_inc(x0_in, 16)
            sp.dma_start(gate_sb[:, :], gate_w).then_inc(gate_in, 16)
            for c in range(E // W_CHUNK):
                es = slice(c * W_CHUNK, (c + 1) * W_CHUNK)
                sp.dma_start(w1_sb[:, es, :], w1[es].rearrange("e c f -> c e f")).then_inc(w1_in[c], 16)
                sp.dma_start(w2_sb[:, es, :, :], w2[es].rearrange("e (k p) c -> p e k c", p=P)).then_inc(w2_in[c], 16)
            sp.dma_start(x_all[:, PAIR_TILES:, :], x_rows[:, PAIR_TILES:, :]).then_inc(x_in, 16)

            def body(st):
                if st.ffn2:
                    sp.wait_ge(combined, st.ffn_before + len(st.steps))
                    t = st.pair(1) * PAIR_TILES
                    sp.dma_start(out_rows[:, bass.ds(t, PAIR_TILES), :],
                                 x_all[:, bass.ds(t, PAIR_TILES), :]).then_inc(out_done, 16)
            iterations(sp, body)
            sp.wait_ge(out_done, 16 * PAIRS)

        @block.gpsimd
        def _(pool):
            pool.memset(ident[:, :], 0.0).then_inc(ident_zero, 1)
            pool.wait_ge(ident_zero, 1)
            pool.affine_select(out=ident[:, :], in_=ident[:, :], compare_op=ALU.not_equal, fill=1.0,
                               base=0, pattern=[[-1, P]], channel_multiplier=1).then_inc(ident_ready, 1)
            pool.iota(expert_ids[:, :], [[1, E]], base=0, channel_multiplier=0,
                      allow_small_or_imprecise_dtypes=True).then_inc(ident_ready, 1)

            def body(st):
                for slot in range(st.slots):
                    for q, at in st.seq_tasks(slot):
                        k = st.unit(at - SCAN_LAG)
                        if k is not None:
                            u = (st.seqs_before + q) * UNITS + k
                            pool.wait_ge(scan_done, u + 1)
                            pool.wait_ge(front_read, st.front(st.unit_places[k], q) + 1)
                            if some(u - 1):
                                pool.wait_ge(sum_done, u - 1)
                            pool.tensor_tensor(prod[:, k % 2], state[:, k % 2],
                                               cs[:, k % 2].unsqueeze(2).broadcast_to([P, 2, HALVES, SEQ]),
                                               ALU.mult).then_inc(prod_ready, 1)
                            pool.wait_ge(prod_ready, u + 1)
                            pool.tensor_tensor(prod[:, k % 2, 0], prod[:, k % 2, 0], prod[:, k % 2, 1],
                                               ALU.add).then_inc(prod_added, 1)
            iterations(pool, body)

        @block.scalar
        def _(act):
            act.dma_start(inproj_sb[:, :], in_proj_w).then_inc(small_in, 16)
            act.dma_start(taps_sb[:, :, :], conv_w.rearrange("d o k -> (o d) k").partition_broadcast(P)).then_inc(small_in, 16)
            act.dma_start(normw_sb[:, :], norm_w.rearrange("(p o) -> p o", o=1)).then_inc(small_in, 16)
            with nc.allow_non_contiguous_dma(reason="vectors of 256 over partitions"):
                act.dma_start(convb_sb[:, :], conv_b.rearrange("(h p) -> p h", p=P)).then_inc(small_in, 16)
                act.dma_start(dtb_sb[:, :], dt_proj_b.rearrange("(h p) -> p h", p=P)).then_inc(small_in, 16)
                act.dma_start(d_sb[:, :], D.rearrange("(h p) -> p h", p=P)).then_inc(small_in, 16)
            act.dma_start(alog_sb[:, :, :], A_log.rearrange("(h p) n -> p h n", p=P)).then_inc(small_in, 16)
            act.dma_start(xproj_sb[:, :, :], x_proj_w.rearrange("(h p) n -> p h n", p=P)).then_inc(small_in, 16)
            act.dma_start(dtproj_sb[:, :], dt_proj_w).then_inc(small_in, 16)
            act.dma_start(outproj_sb[:, :, :], out_proj_w.rearrange("(h p) n -> p h n", p=P)).then_inc(small_in, 16)
            act.dma_start(xbc_sb[:, :, 0, :], x_proj_w[:, RANK:XP].rearrange("(h p) n -> p h n", p=P)).then_inc(small_in, 16)
            loaded = [None]

            def tables(name):
                if loaded[0] != name:
                    act.preload_act_table_set(name)
                loaded[0] = name

            def router_exp(r):
                tables("natural_log_exp_and_others")
                act.wait_ge(gap_ready, r + 1)
                act.activation(top_exp[:, :], top_gap[:, :], ACT.Exp).then_inc(gap_exp_ready, 1)

            router_exp(0)
            act.wait_ge(small_in, 16 * SMALL_DMAS)
            act.activation(a_sb[:, :, :], alog_sb[:, :, :], ACT.Exp).then_inc(a_exp_ready, 1)


            def body(st):
                loaded[0] = None
                if isinstance(st.j, int) and st.j == 1:
                    act.wait_ge(a_ready, 1)
                for slot in range(st.slots):
                    if slot in st.l1:
                        i = st.l1[slot]
                        f = st.ffn_before + i
                        tables("gelu_and_others")
                        if some(f - 1):
                            act.wait_ge(o_full, f - 1)
                        for g in range(2):
                            act.wait_ge(h_full, 2 * f + g + 1)
                            act.activation(hT[:, i % 2, 2 * g:2 * g + 2, :], hP[:, g], ACT.Gelu).then_inc(gelu_done, 1)
                    for q, at in st.seq_tasks(slot):
                        m = st.seqs_before + q
                        if at == CONV:
                            tables("silu_and_others")
                            act.wait_ge(front_full, st.front(at, q) + 1)
                            if some(m - 1):
                                act.wait_ge(y_ready, m - 1)
                            for h in range(HALVES):
                                ins = act.activation(xi[:, q, h, :], front[:, h * SEQ:(h + 1) * SEQ], ACT.Silu,
                                                     bias=convb_sb[:, h:h + 1])
                            ins.then_inc(front_read, 1)
                            act.wait_ge(b_full, st.b_bank(at, q) + 1)
                            act.activation(sres[:, q, :, :], bP[:, :, :], ACT.Silu).then_inc(b_read, 1)
                        if at == DTPROJ + 1:
                            tables("natural_log_exp_and_others")
                            act.wait_ge(sp_arg, 2 * m + 1)
                            act.activation(ez[:, :, :], zneg[:, :, :], ACT.Exp).then_inc(sp_act, 1)
                            act.wait_ge(sp_arg, 2 * m + 2)
                            act.activation(lnz[:, :, :], ez1[:, :, :], ACT.Ln).then_inc(sp_act, 1)
                        k = st.unit(at)
                        if k is not None:
                            u = m * UNITS + k
                            act.wait_ge(front_full, st.front(at, q) + 1)
                            if some(u - 1):
                                act.wait_ge(prod_ready, u - 1)
                            act.activation(cs[:, k % 2], front[:, :].rearrange("p (n t) -> p n t", n=2),
                                           ACT.Copy).then_inc(front_read, 1)
                        k = st.unit(at + 1)
                        if k is not None and k % 2 == 0:
                            tables("natural_log_exp_and_others")
                            if k == 0:
                                act.wait_ge(delta_ready, m + 1)
                            for kk in (k, k + 1):
                                u = m * UNITS + kk
                                if some(u - NDA + 1):
                                    act.wait_ge(scan_done, u - NDA + 1)
                                for n in range(2):
                                    for h in range(HALVES):
                                        ins = act.activation(dA[:, kk % NDA, n, h, 1:SEQ], delta[:, h, 1:SEQ], ACT.Exp,
                                                             scale=a_sb[:, h, 2 * kk + n:2 * kk + n + 1])
                                ins.then_inc(dA_ready, 1)
                    for r, (_, _, at, _, _) in enumerate(st.routes):
                        if slot == at:
                            router_exp(st.routes_before + r)
            iterations(act, body)

        @block.vector
        def _(dve):
            def rsqrt(dst, src, eps):
                n = slice(0, src.shape[1])
                dve.tensor_scalar(rs_in[:, n], src, eps, None, ALU.add)
                dve.drain()
                dve.tensor_scalar(rs_int[:, n], rs_in[:, n].bitcast(I32), 1, None, ALU.logical_shift_right)
                dve.tensor_scalar(rs_half[:, n], rs_in[:, n], -0.5, None, ALU.mult)
                dve.drain()
                dve.tensor_scalar(dst.bitcast(I32), rs_int[:, n], -1.0, RSQRT_GUESS, ALU.mult, ALU.add)
                dve.drain()
                for _ in range(3):
                    dve.tensor_tensor(rs_t[:, n], dst, dst, ALU.mult)
                    dve.drain()
                    dve.tensor_tensor(rs_t[:, n], rs_t[:, n], rs_half[:, n], ALU.mult)
                    dve.drain()
                    dve.scalar_tensor_tensor(dst, rs_t[:, n], 1.5, dst, ALU.add, ALU.mult)
                    dve.drain()

            def mean_and_var(t0, n):
                dve.drain()
                for i in range(n):
                    dve.bn_stats(stats[:, i, :], x_all[:, bass.ds(t0 + i, 1), :].squeeze(1))
                dve.drain()
                for i in range(n):
                    dve.bn_aggr(moments[:, i, :], stats[:, i, :])
                dve.drain()

            def normalise(t0):
                mean_and_var(t0, PAIR_TILES)
                rsqrt(rstd[:, :], moments[:, :, 1], EPS)
                for i in range(PAIR_TILES):
                    ins = dve.tensor_scalar(route_rows[:, i, :], x_all[:, bass.ds(t0 + i, 1), :].squeeze(1),
                                            moments[:, i, 0:1], rstd[:, i:i + 1], ALU.subtract, ALU.mult)
                ins.then_inc(route_rows_ready, 1)

            def normalise_seqs(t0):
                xs = x_all[:, bass.ds(t0, PAIR_TILES), :]
                mean_and_var(t0, PAIR_TILES)
                rsqrt(rstd[:, :], moments[:, :, 1], EPS)
                dve.tensor_tensor(rms_in[:, :], rstd[:, :], rstd[:, :], ALU.mult)
                for i in range(PAIR_TILES):
                    dve.tensor_scalar(lrow[:, i, :], x_all[:, bass.ds(t0 + i, 1), :].squeeze(1),
                                      moments[:, i, 0:1], rstd[:, i:i + 1], ALU.subtract, ALU.mult)
                dve.drain()
                dve.tensor_tensor(rms_in[:, :], rms_in[:, :], moments[:, :, 1], ALU.mult)
                dve.tensor_tensor(xs, xs, lrow[:, :, :], ALU.add)
                dve.drain()
                rsqrt(rstd2[:, :], rms_in[:, :], EPS)
                for i in range(PAIR_TILES):
                    ins = dve.tensor_scalar(seq_rows[:, i, :], lrow[:, i, :], rstd2[:, i:i + 1], None, ALU.mult)
                ins.then_inc(seq_rows_ready, 1)

            def take_rows(s, use):
                dve.wait_ge(front_full, use + 1)
                dve.tensor_copy(lnT_hi[s][:, :], front[:, :])
                dve.tensor_copy(lnT[:, :], front[:, :]).then_inc(front_read, 1)
                dve.drain()
                dve.tensor_tensor(lnT_lo[s][:, :], lnT[:, :], lnT_hi[s][:, :].bitcast(F32), ALU.subtract).then_inc(lnT_ready, 1)

            def take_logits(use):
                dve.wait_ge(front_full, use + 1)
                dve.tensor_copy(logits[:, :, :].rearrange("p t e -> p (t e)"),
                                front[:, 0:PAIR_TILES * E]).then_inc(front_read, 1)
                dve.drain()
                for i in range(PAIR_TILES):
                    dve.max(top[:, i, :], logits[:, i, :])
                dve.drain()
                dve.tensor_tensor(top_gap[:, :], top[:, :, 1], top[:, :, 0], ALU.subtract).then_inc(gap_ready, 1)
                for i in range(PAIR_TILES):
                    dve.max_index(top_at[:, i, :], top[:, i, :], logits[:, i, :])
                dve.drain()
                dve.tensor_copy(top_atf[:, :, :], top_at[:, :, 0:2])

            def expert_weights(s, r):
                dve.wait_ge(gap_exp_ready, r + 1)
                dve.tensor_scalar(top_sum[:, :], top_exp[:, :], 1.0, None, ALU.add)
                dve.drain()
                dve.reciprocal(top_sum[:, :], top_sum[:, :])
                dve.drain()
                dve.tensor_scalar(top_w[:, :, 0], top_sum[:, :], 0.5, None, ALU.mult)
                dve.scalar_tensor_tensor(top_w[:, :, 1], top_exp[:, :], 0.5, top_sum[:, :], ALU.mult, ALU.mult)
                full = [P, PAIR_TILES, E]
                for k in range(2):
                    dve.tensor_tensor(onehot[:, k], expert_ids[:, :].unsqueeze(1).broadcast_to(full),
                                      top_atf[:, :, k:k + 1].broadcast_to(full), ALU.is_equal)
                dve.drain()
                for k in range(2):
                    dve.tensor_tensor(onehot[:, k], onehot[:, k], top_w[:, :, k:k + 1].broadcast_to(full), ALU.mult)
                dve.drain()
                dve.tensor_tensor(combine_w[s][:, :, :], onehot[:, 0], onehot[:, 1], ALU.add)
                dve.drain()

            def split_w1(c):
                es = slice(c * W_CHUNK, (c + 1) * W_CHUNK)
                dve.wait_ge(w1_in[c], 16)
                dve.tensor_copy(w1_hi[:, es, :], w1_sb[:, es, :])
                dve.drain()
                dve.tensor_tensor(w1_lo[:, es, :], w1_sb[:, es, :], w1_hi[:, es, :].bitcast(F32),
                                  ALU.subtract).then_inc(w1_split, 1)

            dve.wait_ge(x0_in, 16)
            normalise(0)
            take_rows(0, 0)
            split_w1(0)
            dve.wait_ge(ident_ready, 2)
            take_logits(1)
            expert_weights(0, 0)
            for c in range(1, E // W_CHUNK):
                split_w1(c)
            dve.drain()

            def ssm_weights():
                dve.wait_ge(small_in, 16 * SMALL_DMAS)
                dve.tensor_scalar(inproj_sb[:, :], inproj_sb[:, :], normw_sb[:, 0:1], None, ALU.mult)
                dve.memset(xnT[:, 0:TAPS - 1], 0.0)
                dve.memset(dA[:, :, :, :, 0:1], 0.0)
                dve.drain()
                for k in range(TAPS):
                    dve.tensor_tensor(convw_sb[:, k, :], inproj_sb[:, 0:DI], taps_sb[:, :, k], ALU.mult)
                dve.tensor_copy(resw_sb[:, :], inproj_sb[:, DI:])
                for part in (1, 2):
                    dve.tensor_copy(xbc_sb[:, :, part, :], xbc_sb[:, :, 0, :])
                dve.wait_ge(ident_ready, 2)
                for part in range(3):
                    r = slice(part * BC, (part + 1) * BC)
                    dve.tensor_copy(pick[r], ident[r, r].unsqueeze(2).broadcast_to([BC, BC, P]))
                dve.drain()
                dve.wait_ge(a_exp_ready, 1)
                dve.tensor_scalar(a_sb[:, :, :], a_sb[:, :, :], -1.0, None, ALU.mult).then_inc(a_ready, 1)


            def body(st):
                if isinstance(st.j, int) and st.j == 0:
                    dve.wait_ge(x_in, 16)
                for slot in range(st.slots):
                    for r, (_, at, exp, s, _) in enumerate(st.routes):
                        if slot == at + 1:
                            take_rows(s, st.front("rows", r))
                        if slot == at + 4:
                            take_logits(st.front("logits", r))
                        if slot == exp + 1:
                            expert_weights(s, st.routes_before + r)
                    if slot in st.combine:
                        i = st.combine[slot]
                        s, e = st.steps[i]
                        t0 = st.pair(s) * PAIR_TILES
                        dve.wait_ge(o_full, st.ffn_before + i + 1)
                        if some(st.ffn_before + i):
                            dve.wait_ge(combined, st.ffn_before + i)
                        for t in range(PAIR_TILES):
                            xt = x_all[:, bass.ds(t0 + t, 1), :].squeeze(1)
                            ins = dve.scalar_tensor_tensor(xt, oP[:, i % 2, t, :], combine_w[s][:, t, e:e + 1], xt,
                                                           ALU.mult, ALU.add)
                        ins.then_inc(combined, 1)
                    if slot == st.seq_norm:
                        normalise_seqs(st.j * PAIR_TILES)
                    for q, at in st.seq_tasks(slot):
                        m = st.seqs_before + q
                        t0 = (st.j - 1) * PAIR_TILES + q * SEQ_TILES
                        xs = x_all[:, bass.ds(t0, SEQ_TILES), :]
                        if at == TRANSPOSE + 1:
                            dve.wait_ge(front_full, st.front(TRANSPOSE, q) + 1)
                            dve.tensor_copy(xnT[:, TAPS - 1:], front[:, 0:SEQ]).then_inc(front_read, 1)
                        if at == XPROJ + 1:
                            dve.wait_ge(front_full, st.front(XPROJ, q) + 1)
                            dve.tensor_copy(rank_sb[:, :], front[0:RANK, 0:SEQ])
                            dve.tensor_copy(bc_f[:, :], front[0:3 * BC, SEQ:2 * SEQ])
                            dve.tensor_copy(bc3[:, :], front[0:3 * BC, SEQ:2 * SEQ]).then_inc(front_read, 1)
                            dve.drain()
                            dve.tensor_tensor(bc_f[:, :], bc_f[:, :], bc3[:, :], ALU.subtract)
                            dve.drain()
                            dve.tensor_copy(bc_mid[:, :], bc_f[:, :])
                            dve.drain()
                            dve.tensor_copy(bc3[BC:2 * BC, :], bc_mid[BC:2 * BC, :])
                            dve.tensor_tensor(bc3[2 * BC:3 * BC, :], bc_f[2 * BC:3 * BC, :], bc_mid[2 * BC:3 * BC, :],
                                              ALU.subtract)
                            dve.drain()
                            dve.sem_inc(bc3_ready, 1)
                        if at == DTPROJ + 1:
                            dve.wait_ge(front_full, st.front(DTPROJ, q) + 1)
                            for h in range(HALVES):
                                ins = dve.tensor_scalar(z[:, h, :], front[:, h * SEQ:(h + 1) * SEQ],
                                                        dtb_sb[:, h:h + 1], None, ALU.add)
                            ins.then_inc(front_read, 1)
                            dve.drain()
                            dve.scalar_tensor_tensor(zneg[:, :, :], z[:, :, :], -1.0, z[:, :, :], ALU.mult,
                                                     ALU.min).then_inc(sp_arg, 1)
                            dve.wait_ge(sp_act, 2 * m + 1)
                            dve.tensor_scalar(ez1[:, :, :], ez[:, :, :], 1.0, None, ALU.add).then_inc(sp_arg, 1)
                            dve.drain()
                            dve.scalar_tensor_tensor(ez[:, :, :], ez1[:, :, :], -1.0, ez[:, :, :], ALU.add, ALU.subtract)
                            dve.drain()
                            dve.wait_ge(sp_act, 2 * m + 2)
                            dve.tensor_tensor(lnz[:, :, :], lnz[:, :, :], ez[:, :, :], ALU.subtract)
                            dve.drain()
                            if some(m):
                                dve.wait_ge(dA_ready, m * UNITS)
                            dve.scalar_tensor_tensor(delta[:, :, :], z[:, :, :], 0.0, lnz[:, :, :], ALU.max,
                                                     ALU.add).then_inc(delta_ready, 1)
                            dve.drain()
                            dve.tensor_tensor(udx[:, :, :], delta[:, :, :], xi[:, q, :, :], ALU.mult)
                            dve.drain()
                        k = st.unit(at)
                        if k is not None:
                            shape = [P, 2, HALVES, SEQ]
                            u = m * UNITS + k
                            dve.wait_ge(b_full, st.b_bank(at, q) + 1)
                            if some(u - NDBU + 1):
                                dve.wait_ge(scan_done, u - NDBU + 1)
                            dve.tensor_tensor(dBu[:, k % NDBU], udx[:, :, :].unsqueeze(1).broadcast_to(shape),
                                              bP[:, :, :].unsqueeze(2).broadcast_to(shape), ALU.mult).then_inc(b_read, 1)
                        k = st.unit(at - SCAN_LAG)
                        if k is not None:
                            u = m * UNITS + k
                            dve.wait_ge(b_read, st.b_bank(at - SCAN_LAG, q) + 1)
                            dve.wait_ge(dA_ready, u + 1)
                            if some(u - 1):
                                dve.wait_ge(prod_ready, u - 1)
                            dve.tensor_tensor_scan(state[:, k % 2].rearrange("p n h t -> p (n h t)"),
                                                   dA[:, k % NDA].rearrange("p n h t -> p (n h t)"),
                                                   dBu[:, k % NDBU].rearrange("p n h t -> p (n h t)"),
                                                   0.0, ALU.mult, ALU.add).then_inc(scan_done, 1)
                        k = st.unit(at - SUM_LAG)
                        if k is not None:
                            u = m * UNITS + k
                            dve.wait_ge(prod_added, u + 1)
                            if some(u):
                                dve.wait_ge(sum_done, u)
                            if k == 0:
                                if some(m):
                                    dve.wait_ge(y_ready, m)
                                for h in range(HALVES):
                                    ins = dve.scalar_tensor_tensor(ysum[:, h, :], xi[:, q, h, :], d_sb[:, h:h + 1],
                                                                   prod[:, k % 2, 0, h], ALU.mult, ALU.add)
                            else:
                                ins = dve.tensor_tensor(ysum[:, :, :], ysum[:, :, :], prod[:, k % 2, 0], ALU.add)
                            ins.then_inc(sum_done, 1)
                        if at == st.yfin:
                            dve.wait_ge(sum_done, (m + 1) * UNITS)
                            dve.tensor_tensor(yT[:, :, :], ysum[:, :, :], sres[:, q], ALU.mult).then_inc(y_ready, 1)
                        if at == st.outp + 1:
                            dve.wait_ge(front_full, st.front(st.outp, q) + 1)
                            dve.tensor_tensor(xs, xs, front[:, 0:SEQ_TILES * C].rearrange("p (t c) -> p t c", c=C),
                                              ALU.add).then_inc(front_read, 1)
                            dve.drain()
                    for norm, _, _, _, ahead in st.routes:
                        if slot == norm:
                            normalise((st.j + ahead) * PAIR_TILES)
            ssm_weights()
            dve.sem_inc(ssm_weights_ready, 1)
            iterations(dve, body)

        @block.tensor
        def _(pe):
            pe.wait_ge(ident_ready, 2)

            def transpose_rows(r, use):
                pe.wait_ge(route_rows_ready, r + 1)
                if some(use):
                    pe.wait_ge(front_read, use)
                for t in range(PAIR_TILES):
                    ins = pe.transpose(front[:, t * P:(t + 1) * P], route_rows[:, t, :], ident[:, :])
                ins.then_inc(front_full, 1)

            def router_logits(r, use):
                pe.wait_ge(front_read, use)
                pe.wait_ge(lnT_ready, r + 1)
                for t in range(PAIR_TILES):
                    ins = pe.matmul(front[:, t * E:(t + 1) * E], lnT[:, t * P:(t + 1) * P], gate_sb[:, :],
                                    start=True, stop=True)
                ins.then_inc(front_full, 1)

            transpose_rows(0, 0)
            pe.wait_ge(gate_in, 16)
            router_logits(0, 1)

            def body(st):
                if isinstance(st.j, int) and st.j == 1:
                    pe.wait_ge(ssm_weights_ready, 1)
                for slot in range(st.slots):
                    if slot in st.l1:
                        i = st.l1[slot]
                        s, e = st.steps[i]
                        f = st.ffn_before + i
                        first_use = isinstance(st.j, int) and st.j == 0
                        if first_use and e % W_CHUNK == 0:
                            pe.wait_ge(w1_split, e // W_CHUNK + 1)
                        if e == 0:
                            pe.wait_ge(lnT_ready, st.routes_before + s)
                        for g in range(2):
                            if some(2 * f + g - 1):
                                pe.wait_ge(gelu_done, 2 * f + g - 1)
                            for k in range(2):
                                c0 = (2 * g + k) * P
                                pe.matmul(hP[:, g, k, :], w1_hi[:, e, c0:c0 + P], lnT_hi[s][:, :], start=True, stop=False)
                                pe.matmul(hP[:, g, k, :], w1_hi[:, e, c0:c0 + P], lnT_lo[s][:, :], start=False, stop=False)
                                ins = pe.matmul(hP[:, g, k, :], w1_lo[:, e, c0:c0 + P], lnT_hi[s][:, :], start=False, stop=True)
                            ins.then_inc(h_full, 1)
                    if slot in st.l2:
                        i = st.l2[slot]
                        s, e = st.steps[i]
                        f = st.ffn_before + i
                        if isinstance(st.j, int) and st.j == 0 and e % W_CHUNK == 0:
                            pe.wait_ge(w2_in[e // W_CHUNK], 16)
                        pe.wait_ge(gelu_done, 2 * f + 2)
                        if some(f - 1):
                            pe.wait_ge(combined, f - 1)
                        for t in range(PAIR_TILES):
                            for k in range(KF):
                                ins = pe.matmul(oP[:, i % 2, t, :], hT[:, i % 2, k, t * P:(t + 1) * P], w2_sb[:, e, k, :],
                                                start=k == 0, stop=k == KF - 1)
                        ins.then_inc(o_full, 1)
                    for r, (_, at, _, _, _) in enumerate(st.routes):
                        if slot == at:
                            transpose_rows(st.routes_before + r, st.front("rows", r))
                    for q, at in st.seq_tasks(slot):
                        m = st.seqs_before + q
                        if at in st.front_places:
                            before = st.front(at, q)
                            k = st.unit(at)
                            if k is not None:
                                u = m * UNITS + k
                                if k == 0:
                                    pe.wait_ge(bc3_ready, m + 1)
                                pe.wait_ge(b_read, st.b_bank(at, q))
                                for n in range(2):
                                    ins = pe.matmul(bP[:, n, :], pick[:, 2 * k + n, :], bc3[:, :],
                                                    start=True, stop=True)
                                ins.then_inc(b_full, 1)
                            if some(before):
                                pe.wait_ge(front_read, before)
                            if at == TRANSPOSE:
                                pe.wait_ge(seq_rows_ready, st.j)
                                for t in range(SEQ_TILES):
                                    ins = pe.transpose(front[:, t * P:(t + 1) * P], seq_rows[:, q * SEQ_TILES + t, :], ident[:, :])
                            elif at == CONV:
                                for h in range(HALVES):
                                    for k in range(TAPS):
                                        ins = pe.matmul(front[:, h * SEQ:(h + 1) * SEQ], convw_sb[:, k, h * P:(h + 1) * P],
                                                        xnT[:, k:k + SEQ], start=k == 0, stop=k == TAPS - 1)
                            elif at == XPROJ:
                                for h in range(HALVES):
                                    ins = pe.matmul(front[0:RANK, 0:SEQ], xproj_sb[:, h, 0:RANK], xi[:, q, h, :],
                                                    start=h == 0, stop=h == HALVES - 1)
                                for h in range(HALVES):
                                    ins = pe.matmul(front[0:3 * BC, SEQ:2 * SEQ],
                                                    xbc_sb[:, h].rearrange("p r n -> p (r n)"), xi[:, q, h, :],
                                                    start=h == 0, stop=h == HALVES - 1)
                            elif at == DTPROJ:
                                for h in range(HALVES):
                                    ins = pe.matmul(front[:, h * SEQ:(h + 1) * SEQ], dtproj_sb[:, h * P:(h + 1) * P],
                                                    rank_sb[:, :], start=True, stop=True)
                            elif at == st.outp:
                                pe.wait_ge(y_ready, m + 1)
                                for t in range(SEQ_TILES):
                                    for h in range(HALVES):
                                        ins = pe.matmul(front[:, t * C:(t + 1) * C], yT[:, h, t * P:(t + 1) * P],
                                                        outproj_sb[:, h, :], start=h == 0, stop=h == HALVES - 1)
                            else:
                                for n in range(2):
                                    ins = pe.matmul(front[:, n * SEQ:(n + 1) * SEQ], pick[:, NST + 2 * k + n, :],
                                                    bc3[:, :], start=True, stop=True)
                            ins.then_inc(front_full, 1)
                            if at == CONV:
                                if some(st.b_bank(at, q)):
                                    pe.wait_ge(b_read, st.b_bank(at, q))
                                for h in range(HALVES):
                                    ins = pe.matmul(bP[:, h, :], resw_sb[:, h * P:(h + 1) * P], xnT[:, TAPS - 1:],
                                                    start=True, stop=True)
                                ins.then_inc(b_full, 1)
                    for r, (_, at, _, _, _) in enumerate(st.routes):
                        if slot == at + 3:
                            router_logits(st.routes_before + r, st.front("logits", r))
            iterations(pe, body)


_INS = ["L0_attn_x", "L0_attn_in_proj_w", "L0_attn_conv_w", "L0_attn_conv_b", "L0_attn_x_proj_w",
        "L0_attn_dt_proj_w", "L0_attn_dt_proj_b", "L0_attn_A_log", "L0_attn_D", "L0_attn_out_proj_w",
        "L0_attn_norm_w", "L0_ffn_gate_w", "L0_ffn_w1", "L0_ffn_w2"]


def kernel(**inputs):
    import numpy as _np
    import concourse.bacc as _bacc
    from concourse import mybir as _mybir
    from concourse.bass_utils import run_bass_kernel_spmd as _run

    nc = _bacc.Bacc("TRN2", target_bir_lowering=False, num_devices=1)
    arrays, args = {}, []
    for name in _INS:
        a = _np.ascontiguousarray(inputs[name])
        arrays[f"in_{name}"] = a
        args.append(nc.dram_tensor(f"in_{name}", a.shape, _mybir.dt.from_np(a.dtype), kind="ExternalInput").ap())
    out = nc.dram_tensor("out", (BATCH, SEQ, C), F32, kind="ExternalOutput").ap()
    macaron_mamba_moe(nc, *args, out)
    r = _run(nc, [arrays], core_ids=[0])
    return r.results[0]["out"]
```

```python
import concourse.bass as bass
from concourse import mybir
from contextlib import ExitStack

F32 = mybir.dt.float32
F32R = mybir.dt.float32r
BF16 = mybir.dt.bfloat16
I32 = mybir.dt.int32
U32 = mybir.dt.uint32
ALU = mybir.AluOpType
ACT = mybir.ActivationFunctionType

P = 128
BATCH, SEQ, C = 16, 256, 128
E, F = 8, 512
DI, NST, RANK, TAPS = 256, 16, 64, 4
W_CHUNK = 2
EPS = 1e-5
RSQRT_GUESS = float(0x5F3759DF)

TILES = BATCH * SEQ // P
PAIR_TILES = 4
PAIRS = TILES // PAIR_TILES
SEQ_TILES = SEQ // P
TOK = PAIR_TILES * P
KF = F // P
HALVES = DI // P
XP = RANK + 2 * NST
BC = 2 * NST
UNITS = NST // 2

WEIGHTS_SLOT = 9

FIRST_FULL, END_FULL, LAST = 2, PAIRS - 1, PAIRS + 1

SEQ_START = (0, 13)
SEQ_START_ONE_FFN = (1, 14)
TRANSPOSE, CONV, XPROJ, DTPROJ = 0, 1, 3, 4
UNIT_PLACES = tuple(6 + 3 * (k // 2) + k % 2 for k in range(UNITS))
NORM_LAG = {"route": 1, "seq": 3}
SCAN_LAG, SUM_LAG = 1, 3
YFIN = UNIT_PLACES[-1] + SUM_LAG + 1
OUTP = YFIN + 1
SEQ_END = OUTP + 1
FRONT_PLACES = (TRANSPOSE, CONV, XPROJ, DTPROJ, *UNIT_PLACES, OUTP)
FRONT_USES = len(FRONT_PLACES)
B_USES = 1 + UNITS


def unit(place):
    return UNIT_PLACES.index(place) if place in UNIT_PLACES else None


class Stages:

    def __init__(self, j, ffn1, ssm, ffn2, next_route):
        self.j, self.ffn1, self.ssm, self.ffn2 = j, ffn1, ssm, ffn2
        self.seq_start = SEQ_START if ffn1 and ffn2 else SEQ_START_ONE_FFN
        order = sorted([(e, 0, e) for e in range(E) if ffn1] + [(e + 3.5, 1, e) for e in range(E) if ffn2])
        self.steps = [(s, e) for _, s, e in order]
        lead = 0 if ffn1 else 2
        self.l1 = {2 * (i + lead): i for i in range(len(self.steps))}
        self.l2 = {slot + 3: i for slot, i in self.l1.items()}
        self.combine = {slot + 4: i for slot, i in self.l1.items()}
        self.routes = [(0, 5, 11, 1, -2) if ffn1 else (0, 3, 7, 1, -2)] if ffn2 else []
        self.seq_norm = None
        if ffn1:
            last = [slot for slot, i in self.l1.items() if self.steps[i][0] == 0][-1]
            self.seq_norm = last + 5
            if next_route:
                rows, exp = (last + 2, last + 7) if ffn2 else (25, 29) if ssm else (last + 3, last + 7)
                self.routes.append((last - 5, rows, exp, 0, 1))
        self.norms = sorted([(at, "route", ahead) for at, _, _, _, ahead in self.routes]
                            + ([(self.seq_norm, "seq", 0)] if ffn1 else []))
        ends = [max(self.combine) + 1] + ([self.seq_start[1] + SEQ_END + 1] if ssm else [])
        ends += [exp + 2 for _, _, exp, _, _ in self.routes]
        self.slots = max(ends + [self.seq_norm + NORM_LAG["seq"] + 1 if ffn1 else 0])
        edge = {0: (0, 1, 1), 1: (E, 2, 3), PAIRS: (2 * E * (PAIRS - 1), 2 * PAIRS - 2, 3 * PAIRS - 2),
                LAST: (2 * E * PAIRS - E, 2 * PAIRS - 1, 3 * PAIRS - 1)}
        full = (2 * E * (j - 1), 2 * j - 1, 3 * j - 1)
        self.ffn_before, self.routes_before, self.norms_before = edge.get(j, full) if isinstance(j, int) else full
        self.seqs_before = 2 * (j - 1) if not isinstance(j, int) or j else 0
        self.front_before = 2 * self.routes_before + FRONT_USES * self.seqs_before
        order = []
        for slot in range(self.slots):
            order += [("rows", r) for r, route in enumerate(self.routes) if slot == route[1]]
            order += [(at, q) for q, at in self.seq_tasks(slot) if at in FRONT_PLACES]
            order += [("logits", r) for r, route in enumerate(self.routes) if slot == route[1] + 3]
        self.front_at = {use: n for n, use in enumerate(order)}
        order = [(at, q) for slot in range(self.slots) for q, at in self.seq_tasks(slot)
                 if at == CONV or unit(at) is not None]
        self.b_before = B_USES * self.seqs_before
        self.b_at = {use: n for n, use in enumerate(order)}

    def seq_tasks(self, slot):
        if not self.ssm:
            return []
        return [(q, slot - self.seq_start[q]) for q in range(2) if 0 <= slot - self.seq_start[q] <= SEQ_END]

    def front(self, *use):
        return self.front_before + self.front_at[use]

    def b_bank(self, *use):
        return self.b_before + self.b_at[use]

    def pair(self, stage):
        return self.j - (2 if stage else 0)


def some(count):
    return not isinstance(count, int) or count > 0


def last_user(u, k, buffers):
    before = k - buffers if k >= buffers else max(n for n in range(UNITS) if n % buffers == k) - UNITS
    return u - (k - before) + 1


def macaron_mamba_moe(nc, x, in_proj_w, conv_w, conv_b, x_proj_w, dt_proj_w, dt_proj_b, A_log, D,
                      out_proj_w, norm_w, gate_w, w1, w2, out):
    ctx = ExitStack()
    with ctx:
        def sb(name, shape, dt=F32):
            return ctx.enter_context(nc.sbuf_tensor(name, shape, dt))

        def ps(name, shape):
            return ctx.enter_context(nc.psum_tensor(name, shape, F32))

        def sem(name):
            return ctx.enter_context(nc.semaphore(name))

        x_rows = x.rearrange("b (s p) c -> p (b s) c", p=P)
        out_rows = out.rearrange("b (s p) c -> p (b s) c", p=P)

        x_all = sb("x_all", [P, TILES, C])
        w1_hi = sb("w1_hi", [P, E, F], F32R)
        w1_lo = sb("w1_lo", [P, E, F], F32R)
        w2_sb = sb("w2_sb", [P, E, KF, C])
        gate_sb = sb("gate_sb", [P, E])
        inproj_sb = sb("inproj_sb", [P, 2 * DI])
        taps_sb = sb("taps_sb", [P, DI, TAPS])
        normw_sb = sb("normw_sb", [P, 1])
        convw_sb = sb("convw_sb", [P, TAPS, DI])
        resw_sb = sb("resw_sb", [P, DI])
        convb_sb = sb("convb_sb", [P, HALVES])
        dtb_sb = sb("dtb_sb", [P, HALVES])
        d_sb = sb("d_sb", [P, HALVES])
        alog_sb = sb("alog_sb", [P, HALVES, NST])
        a_sb = sb("a_sb", [P, HALVES, NST])
        xproj_sb = sb("xproj_sb", [P, HALVES, XP])
        xbc_sb = sb("xbc_sb", [P, HALVES, 3, BC])
        dtproj_sb = sb("dtproj_sb", [RANK, DI])
        outproj_sb = sb("outproj_sb", [P, HALVES, C])
        ident = sb("ident", [P, P])
        pick = sb("pick", [3 * BC, BC, P], BF16)
        expert_ids = sb("expert_ids", [P, E])
        route_rows = sb("route_rows", [P, PAIR_TILES, C])
        seq_rows = sb("seq_rows", [P, PAIR_TILES, C])
        stats = sb("stats", [P, PAIR_TILES, 6])
        route_moments = sb("route_moments", [P, PAIR_TILES, 2])
        seq_moments = sb("seq_moments", [P, PAIR_TILES, 2])
        rs_in = sb("rs_in", [P, 2 * PAIR_TILES])
        eps_sb = sb("eps_sb", [P, PAIR_TILES])
        rs_half = sb("rs_half", [P, 2 * PAIR_TILES])
        rs_t = sb("rs_t", [P, 2 * PAIR_TILES])
        route_rstd = sb("route_rstd", [P, PAIR_TILES])
        seq_scales = sb("seq_scales", [P, 2 * PAIR_TILES])
        lnT = sb("lnT", [P, TOK])
        lnT_hi = [sb(f"lnT_hi{s}", [P, TOK], F32R) for s in range(2)]
        lnT_lo = [sb(f"lnT_lo{s}", [P, TOK], F32R) for s in range(2)]
        combine_w = [sb(f"combine_w{s}", [P, PAIR_TILES, E]) for s in range(2)]
        logits = sb("logits", [P, PAIR_TILES, E])
        top = sb("top", [P, PAIR_TILES, 8])
        top_at = sb("top_at", [P, PAIR_TILES, 8], U32)
        top_atf = sb("top_atf", [P, PAIR_TILES, 2])
        top_gap = sb("top_gap", [P, PAIR_TILES])
        top_exp = sb("top_exp", [P, PAIR_TILES])
        top_sum = sb("top_sum", [P, PAIR_TILES])
        top_w = sb("top_w", [P, PAIR_TILES, 2])
        onehot = sb("onehot", [P, 2, PAIR_TILES, E])
        hT = sb("hT", [P, 2, KF, TOK])
        xnT = sb("xnT", [P, TAPS - 1 + SEQ])
        lrow = sb("lrow", [P, PAIR_TILES, C])
        xi = sb("xi", [P, 2, HALVES, SEQ])
        sres = sb("sres", [P, 2, HALVES, SEQ])
        rank_sb = sb("rank_sb", [RANK, SEQ])
        bc_f = sb("bc_f", [3 * BC, SEQ])
        bc_mid = sb("bc_mid", [3 * BC, SEQ], BF16)
        bc3 = sb("bc3", [3 * BC, SEQ], BF16)
        z = sb("z", [P, HALVES, SEQ])
        zneg = sb("zneg", [P, HALVES, SEQ])
        ez = sb("ez", [P, HALVES, SEQ])
        ez1 = sb("ez1", [P, HALVES, SEQ])
        lnz = sb("lnz", [P, HALVES, SEQ])
        delta = sb("delta", [P, HALVES, SEQ])
        udx = sb("udx", [P, HALVES, SEQ])
        NDA = 4
        dA = sb("dA", [P, NDA, 2, HALVES, SEQ])
        w1_sb = dA[:, :, :, :, :].rearrange("p u n h t -> p (u n h t)").rearrange("p (e f) -> p e f", e=E)
        NDBU = 3
        dBu = sb("dBu", [P, NDBU, 2, HALVES, SEQ])
        NSTATE = 2
        state = sb("state", [P, NSTATE, 2, HALVES, SEQ])
        NCS = 3
        cs = sb("cs", [P, NCS, 2, SEQ])
        NPROD = 3
        prod = sb("prod", [P, NPROD, 2, HALVES, SEQ])
        ysum = sb("ysum", [P, HALVES, SEQ])
        yT = sb("yT", [P, HALVES, SEQ])

        hP = ps("hP", [P, 2, 2, TOK])
        oP = ps("oP", [P, 2, PAIR_TILES, C])
        front = ps("front", [P, TOK])
        bP = ps("bP", [P, 2, SEQ])

        x0_in = sem("x0_in")
        x_in = sem("x_in")
        gate_in = sem("gate_in")
        w1_in = [sem(f"w1_in{c}") for c in range(E // W_CHUNK)]
        w2_in = [sem(f"w2_in{c}") for c in range(E // W_CHUNK)]
        w1_split = sem("w1_split")
        small_in = sem("small_in")
        ident_ready = sem("ident_ready")
        ident_zero = sem("ident_zero")
        a_exp_ready = sem("a_exp_ready")
        a_ready = sem("a_ready")
        ssm_weights_ready = sem("ssm_weights_ready")
        moments_ready = sem("moments_ready")
        scales_ready = sem("scales_ready")
        route_rows_ready = sem("route_rows_ready")
        seq_rows_ready = sem("seq_rows_ready")
        lnT_ready = sem("lnT_ready")
        front_full = sem("front_full")
        front_read = sem("front_read")
        gap_ready = sem("gap_ready")
        gap_exp_ready = sem("gap_exp_ready")
        h_full = sem("h_full")
        gelu_done = sem("gelu_done")
        o_full = sem("o_full")
        combined = sem("combined")
        sp_arg = sem("sp_arg")
        sp_act = sem("sp_act")
        delta_ready = sem("delta_ready")
        dA_ready = sem("dA_ready")
        bc3_ready = sem("bc3_ready")
        b_full = sem("b_full")
        b_read = sem("b_read")
        scan_done = sem("scan_done")
        prod_ready = sem("prod_ready")
        prod_added = sem("prod_added")
        sum_done = sem("sum_done")
        y_ready = sem("y_ready")
        out_done = sem("out_done")

        block = ctx.enter_context(nc.Block())
        SMALL_DMAS = 11

        def iterations(eng, body):
            body(Stages(0, True, False, False, True))
            body(Stages(1, True, True, False, True))
            with eng.Fori(FIRST_FULL, END_FULL) as j:
                body(Stages(j, True, True, True, True))
            body(Stages(PAIRS - 1, True, True, True, False))
            body(Stages(PAIRS, False, True, True, False))
            body(Stages(LAST, False, False, True, False))

        @block.sync
        def _(sp):
            sp.dma_start(x_all[:, 0:PAIR_TILES, :], x_rows[:, 0:PAIR_TILES, :]).then_inc(x0_in, 16)
            sp.dma_start(gate_sb[:, :], gate_w).then_inc(gate_in, 16)
            for c in range(E // W_CHUNK):
                es = slice(c * W_CHUNK, (c + 1) * W_CHUNK)
                sp.dma_start(w1_sb[:, es, :], w1[es].rearrange("e c f -> c e f")).then_inc(w1_in[c], 16)
                sp.dma_start(w2_sb[:, es, :, :], w2[es].rearrange("e (k p) c -> p e k c", p=P)).then_inc(w2_in[c], 16)
            sp.dma_start(x_all[:, PAIR_TILES:, :], x_rows[:, PAIR_TILES:, :]).then_inc(x_in, 16)

            def body(st):
                if st.ffn2:
                    sp.wait_ge(combined, st.ffn_before + len(st.steps))
                    t = st.pair(1) * PAIR_TILES
                    sp.dma_start(out_rows[:, bass.ds(t, PAIR_TILES), :],
                                 x_all[:, bass.ds(t, PAIR_TILES), :]).then_inc(out_done, 16)
            iterations(sp, body)
            sp.wait_ge(out_done, 16 * PAIRS)

        @block.gpsimd
        def _(pool):
            pool.memset(ident[:, :], 0.0).then_inc(ident_zero, 1)
            pool.wait_ge(ident_zero, 1)
            pool.affine_select(out=ident[:, :], in_=ident[:, :], compare_op=ALU.not_equal, fill=1.0,
                               base=0, pattern=[[-1, P]], channel_multiplier=1).then_inc(ident_ready, 1)
            pool.iota(expert_ids[:, :], [[1, E]], base=0, channel_multiplier=0,
                      allow_small_or_imprecise_dtypes=True).then_inc(ident_ready, 1)

            pool.memset(eps_sb[:, :], EPS).then_inc(ident_ready, 1)
            pool.drain()

            def rsqrt(dst, n):
                x, half, t = rs_in[:, 0:n], rs_half[:, 0:n], rs_t[:, 0:n]
                pool.drain()
                pool.tensor_scalar(half, x, -0.5, None, ALU.mult)
                pool.tensor_scalar(dst.bitcast(I32), x.bitcast(I32), -0.5, RSQRT_GUESS, ALU.mult, ALU.add)
                pool.drain()
                for step in range(3):
                    pool.tensor_tensor(t, dst, dst, ALU.mult)
                    pool.drain()
                    pool.tensor_tensor(t, t, half, ALU.mult)
                    pool.drain()
                    pool.tensor_scalar(t, t, 1.5, None, ALU.add)
                    pool.drain()
                    ins = pool.tensor_tensor(dst, t, dst, ALU.mult)
                    if step < 2:
                        pool.drain()
                return ins

            def scales(kind, n):
                pool.wait_ge(moments_ready, n + 1)
                var = (route_moments if kind == "route" else seq_moments)[:, :, 1]
                ones, twos = rs_in[:, 0:PAIR_TILES], rs_in[:, PAIR_TILES:2 * PAIR_TILES]
                pool.tensor_tensor(ones, var, eps_sb[:, :], ALU.add)
                if kind == "route":
                    rsqrt(route_rstd[:, :], PAIR_TILES).then_inc(scales_ready, 1)
                else:
                    pool.drain()
                    pool.tensor_tensor(twos, ones, eps_sb[:, :], ALU.mult)
                    pool.drain()
                    pool.tensor_tensor(twos, twos, var, ALU.add)
                    rsqrt(seq_scales[:, :], 2 * PAIR_TILES).then_inc(scales_ready, 1)

            scales("route", 0)

            def body(st):
                for slot in range(st.slots):
                    for n, (at, kind, _) in enumerate(st.norms):
                        if slot == at:
                            scales(kind, st.norms_before + n)
                    for q, at in st.seq_tasks(slot):
                        k = unit(at - SCAN_LAG)
                        if k is not None:
                            u = (st.seqs_before + q) * UNITS + k
                            pool.wait_ge(scan_done, u + 1)
                            pool.wait_ge(front_read, st.front(UNIT_PLACES[k], q) + 1)
                            if some(last_user(u, k, NPROD)):
                                pool.wait_ge(sum_done, last_user(u, k, NPROD))
                            pool.tensor_tensor(prod[:, k % NPROD], state[:, k % NSTATE],
                                               cs[:, k % NCS].unsqueeze(2).broadcast_to([P, 2, HALVES, SEQ]),
                                               ALU.mult).then_inc(prod_ready, 1)
                            pool.wait_ge(prod_ready, u + 1)
                            pool.tensor_tensor(prod[:, k % NPROD, 0], prod[:, k % NPROD, 0], prod[:, k % NPROD, 1],
                                               ALU.add).then_inc(prod_added, 1)
            iterations(pool, body)

        @block.scalar
        def _(act):
            act.dma_start(inproj_sb[:, :], in_proj_w).then_inc(small_in, 16)
            act.dma_start(taps_sb[:, :, :], conv_w.rearrange("d o k -> (o d) k").partition_broadcast(P)).then_inc(small_in, 16)
            act.dma_start(normw_sb[:, :], norm_w.rearrange("(p o) -> p o", o=1)).then_inc(small_in, 16)
            with nc.allow_non_contiguous_dma(reason="vectors of 256 over partitions"):
                act.dma_start(convb_sb[:, :], conv_b.rearrange("(h p) -> p h", p=P)).then_inc(small_in, 16)
                act.dma_start(dtb_sb[:, :], dt_proj_b.rearrange("(h p) -> p h", p=P)).then_inc(small_in, 16)
                act.dma_start(d_sb[:, :], D.rearrange("(h p) -> p h", p=P)).then_inc(small_in, 16)
            act.dma_start(alog_sb[:, :, :], A_log.rearrange("(h p) n -> p h n", p=P)).then_inc(small_in, 16)
            act.dma_start(xproj_sb[:, :, :], x_proj_w.rearrange("(h p) n -> p h n", p=P)).then_inc(small_in, 16)
            act.dma_start(dtproj_sb[:, :], dt_proj_w).then_inc(small_in, 16)
            act.dma_start(outproj_sb[:, :, :], out_proj_w.rearrange("(h p) n -> p h n", p=P)).then_inc(small_in, 16)
            act.dma_start(xbc_sb[:, :, 0, :], x_proj_w[:, RANK:XP].rearrange("(h p) n -> p h n", p=P)).then_inc(small_in, 16)
            loaded = [None]

            def tables(name):
                if loaded[0] != name:
                    act.preload_act_table_set(name)
                loaded[0] = name

            def router_exp(r):
                tables("natural_log_exp_and_others")
                act.wait_ge(gap_ready, r + 1)
                act.activation(top_exp[:, :], top_gap[:, :], ACT.Exp).then_inc(gap_exp_ready, 1)

            router_exp(0)

            def body(st):
                loaded[0] = None
                if isinstance(st.j, int) and st.j == 1:
                    act.wait_ge(a_ready, 1)
                for slot in range(st.slots):
                    if slot in st.l1:
                        i = st.l1[slot]
                        f = st.ffn_before + i
                        tables("gelu_and_others")
                        if some(f - 1):
                            act.wait_ge(o_full, f - 1)
                        for g in range(2):
                            act.wait_ge(h_full, 2 * f + g + 1)
                            act.activation(hT[:, i % 2, 2 * g:2 * g + 2, :], hP[:, g], ACT.Gelu).then_inc(gelu_done, 1)
                    for q, at in st.seq_tasks(slot):
                        m = st.seqs_before + q
                        if at == CONV:
                            tables("silu_and_others")
                            act.wait_ge(front_full, st.front(at, q) + 1)
                            if some(m - 1):
                                act.wait_ge(y_ready, m - 1)
                            for h in range(HALVES):
                                ins = act.activation(xi[:, q, h, :], front[:, h * SEQ:(h + 1) * SEQ], ACT.Silu,
                                                     bias=convb_sb[:, h:h + 1])
                            ins.then_inc(front_read, 1)
                            act.wait_ge(b_full, st.b_bank(at, q) + 1)
                            act.activation(sres[:, q, :, :], bP[:, :, :], ACT.Silu).then_inc(b_read, 1)
                        if at == DTPROJ + 1:
                            tables("natural_log_exp_and_others")
                            act.wait_ge(sp_arg, 2 * m + 1)
                            act.activation(ez[:, :, :], zneg[:, :, :], ACT.Exp).then_inc(sp_act, 1)
                            act.wait_ge(sp_arg, 2 * m + 2)
                            act.activation(lnz[:, :, :], ez1[:, :, :], ACT.Ln).then_inc(sp_act, 1)
                        k = unit(at)
                        if k is not None:
                            u = m * UNITS + k
                            act.wait_ge(front_full, st.front(at, q) + 1)
                            if some(last_user(u, k, NCS)):
                                act.wait_ge(prod_ready, last_user(u, k, NCS))
                            act.activation(cs[:, k % NCS], front[:, :].rearrange("p (n t) -> p n t", n=2),
                                           ACT.Copy).then_inc(front_read, 1)
                        k = unit(at + 1)
                        if k is not None and k % 2 == 0:
                            tables("natural_log_exp_and_others")
                            if k == 0:
                                act.wait_ge(delta_ready, m + 1)
                            for kk in (k, k + 1):
                                u = m * UNITS + kk
                                if some(last_user(u, kk, NDA)):
                                    act.wait_ge(scan_done, last_user(u, kk, NDA))
                                for n in range(2):
                                    for h in range(HALVES):
                                        ins = act.activation(dA[:, kk % NDA, n, h, 1:SEQ], delta[:, h, 1:SEQ], ACT.Exp,
                                                             scale=a_sb[:, h, 2 * kk + n:2 * kk + n + 1])
                                ins.then_inc(dA_ready, 1)
                    for r, (_, _, at, _, _) in enumerate(st.routes):
                        if slot == at:
                            router_exp(st.routes_before + r)
                    if isinstance(st.j, int) and st.j == 0 and slot == WEIGHTS_SLOT:
                        tables("natural_log_exp_and_others")
                        act.wait_ge(small_in, 16 * SMALL_DMAS)
                        act.activation(a_sb[:, :, :], alog_sb[:, :, :], ACT.Exp).then_inc(a_exp_ready, 1)
            iterations(act, body)

        @block.vector
        def _(dve):
            def mean_and_var(dst, t0):
                dve.drain()
                for i in range(PAIR_TILES):
                    dve.bn_stats(stats[:, i, :], x_all[:, bass.ds(t0 + i, 1), :].squeeze(1))
                dve.drain()
                for i in range(PAIR_TILES):
                    ins = dve.bn_aggr(dst[:, i, :], stats[:, i, :])
                ins.then_inc(moments_ready, 1)

            def normalise(t0, n):
                dve.wait_ge(scales_ready, n + 1)
                for i in range(PAIR_TILES):
                    ins = dve.tensor_scalar(route_rows[:, i, :], x_all[:, bass.ds(t0 + i, 1), :].squeeze(1),
                                            route_moments[:, i, 0:1], route_rstd[:, i:i + 1], ALU.subtract, ALU.mult)
                ins.then_inc(route_rows_ready, 1)

            def normalise_seqs(t0, n):
                xs = x_all[:, bass.ds(t0, PAIR_TILES), :]
                dve.wait_ge(scales_ready, n + 1)
                for rows, scale in ((lrow, 0), (seq_rows, PAIR_TILES)):
                    for i in range(PAIR_TILES):
                        ins = dve.tensor_scalar(rows[:, i, :], x_all[:, bass.ds(t0 + i, 1), :].squeeze(1),
                                                seq_moments[:, i, 0:1], seq_scales[:, scale + i:scale + i + 1],
                                                ALU.subtract, ALU.mult)
                ins.then_inc(seq_rows_ready, 1)
                dve.drain()
                dve.tensor_tensor(xs, xs, lrow[:, :, :], ALU.add)

            def take_rows(s, use):
                dve.wait_ge(front_full, use + 1)
                dve.tensor_copy(lnT_hi[s][:, :], front[:, :])
                dve.tensor_copy(lnT[:, :], front[:, :]).then_inc(front_read, 1)
                dve.drain()
                dve.tensor_tensor(lnT_lo[s][:, :], lnT[:, :], lnT_hi[s][:, :].bitcast(F32), ALU.subtract).then_inc(lnT_ready, 1)

            def take_logits(use):
                dve.wait_ge(front_full, use + 1)
                dve.tensor_copy(logits[:, :, :].rearrange("p t e -> p (t e)"),
                                front[:, 0:PAIR_TILES * E]).then_inc(front_read, 1)
                dve.drain()
                for i in range(PAIR_TILES):
                    dve.max(top[:, i, :], logits[:, i, :])
                dve.drain()
                dve.tensor_tensor(top_gap[:, :], top[:, :, 1], top[:, :, 0], ALU.subtract).then_inc(gap_ready, 1)
                for i in range(PAIR_TILES):
                    dve.max_index(top_at[:, i, :], top[:, i, :], logits[:, i, :])
                dve.drain()
                dve.tensor_copy(top_atf[:, :, :], top_at[:, :, 0:2])

            def expert_weights(s, r):
                dve.wait_ge(gap_exp_ready, r + 1)
                dve.tensor_scalar(top_sum[:, :], top_exp[:, :], 1.0, None, ALU.add)
                dve.drain()
                dve.reciprocal(top_sum[:, :], top_sum[:, :])
                dve.drain()
                dve.tensor_scalar(top_w[:, :, 0], top_sum[:, :], 0.5, None, ALU.mult)
                dve.scalar_tensor_tensor(top_w[:, :, 1], top_exp[:, :], 0.5, top_sum[:, :], ALU.mult, ALU.mult)
                full = [P, PAIR_TILES, E]
                for k in range(2):
                    dve.tensor_tensor(onehot[:, k], expert_ids[:, :].unsqueeze(1).broadcast_to(full),
                                      top_atf[:, :, k:k + 1].broadcast_to(full), ALU.is_equal)
                dve.drain()
                for k in range(2):
                    dve.tensor_tensor(onehot[:, k], onehot[:, k], top_w[:, :, k:k + 1].broadcast_to(full), ALU.mult)
                dve.drain()
                dve.tensor_tensor(combine_w[s][:, :, :], onehot[:, 0], onehot[:, 1], ALU.add)
                dve.drain()

            def split_w1(c):
                es = slice(c * W_CHUNK, (c + 1) * W_CHUNK)
                dve.wait_ge(w1_in[c], 16)
                dve.tensor_copy(w1_hi[:, es, :], w1_sb[:, es, :])
                dve.drain()
                dve.tensor_tensor(w1_lo[:, es, :], w1_sb[:, es, :], w1_hi[:, es, :].bitcast(F32),
                                  ALU.subtract).then_inc(w1_split, 1)

            dve.wait_ge(x0_in, 16)
            mean_and_var(route_moments, 0)
            normalise(0, 0)
            take_rows(0, 0)
            split_w1(0)
            dve.wait_ge(ident_ready, 3)
            take_logits(1)
            expert_weights(0, 0)
            for c in range(1, E // W_CHUNK):
                split_w1(c)
            dve.drain()

            def ssm_weights():
                dve.wait_ge(small_in, 16 * SMALL_DMAS)
                dve.tensor_scalar(inproj_sb[:, :], inproj_sb[:, :], normw_sb[:, 0:1], None, ALU.mult)
                dve.memset(xnT[:, 0:TAPS - 1], 0.0)
                dve.memset(dA[:, :, :, :, 0:1], 0.0)
                dve.drain()
                for k in range(TAPS):
                    dve.tensor_tensor(convw_sb[:, k, :], inproj_sb[:, 0:DI], taps_sb[:, :, k], ALU.mult)
                dve.tensor_copy(resw_sb[:, :], inproj_sb[:, DI:])
                for part in (1, 2):
                    dve.tensor_copy(xbc_sb[:, :, part, :], xbc_sb[:, :, 0, :])
                dve.wait_ge(ident_ready, 3)
                for part in range(3):
                    r = slice(part * BC, (part + 1) * BC)
                    dve.tensor_copy(pick[r], ident[r, r].unsqueeze(2).broadcast_to([BC, BC, P]))
                dve.drain()
                dve.wait_ge(a_exp_ready, 1)
                dve.tensor_scalar(a_sb[:, :, :], a_sb[:, :, :], -1.0, None, ALU.mult).then_inc(a_ready, 1)
                dve.sem_inc(ssm_weights_ready, 1)

            def body(st):
                if isinstance(st.j, int) and st.j == 0:
                    dve.wait_ge(x_in, 16)
                for slot in range(st.slots):
                    for r, (_, at, exp, s, _) in enumerate(st.routes):
                        if slot == at + 1:
                            take_rows(s, st.front("rows", r))
                        if slot == at + 4:
                            take_logits(st.front("logits", r))
                        if slot == exp + 1:
                            expert_weights(s, st.routes_before + r)
                    if slot in st.combine:
                        i = st.combine[slot]
                        s, e = st.steps[i]
                        t0 = st.pair(s) * PAIR_TILES
                        dve.wait_ge(o_full, st.ffn_before + i + 1)
                        if some(st.ffn_before + i):
                            dve.wait_ge(combined, st.ffn_before + i)
                        for t in range(PAIR_TILES):
                            xt = x_all[:, bass.ds(t0 + t, 1), :].squeeze(1)
                            ins = dve.scalar_tensor_tensor(xt, oP[:, i % 2, t, :], combine_w[s][:, t, e:e + 1], xt,
                                                           ALU.mult, ALU.add)
                        ins.then_inc(combined, 1)
                    for q, at in st.seq_tasks(slot):
                        m = st.seqs_before + q
                        t0 = (st.j - 1) * PAIR_TILES + q * SEQ_TILES
                        xs = x_all[:, bass.ds(t0, SEQ_TILES), :]
                        if at == TRANSPOSE + 1:
                            dve.wait_ge(front_full, st.front(TRANSPOSE, q) + 1)
                            dve.tensor_copy(xnT[:, TAPS - 1:], front[:, 0:SEQ]).then_inc(front_read, 1)
                        if at == XPROJ + 1:
                            dve.wait_ge(front_full, st.front(XPROJ, q) + 1)
                            dve.tensor_copy(rank_sb[:, :], front[0:RANK, 0:SEQ])
                            dve.tensor_copy(bc_f[:, :], front[0:3 * BC, SEQ:2 * SEQ])
                            dve.tensor_copy(bc3[:, :], front[0:3 * BC, SEQ:2 * SEQ]).then_inc(front_read, 1)
                            dve.drain()
                            dve.tensor_tensor(bc_f[:, :], bc_f[:, :], bc3[:, :], ALU.subtract)
                            dve.drain()
                            dve.tensor_copy(bc_mid[:, :], bc_f[:, :])
                            dve.drain()
                            dve.tensor_copy(bc3[BC:2 * BC, :], bc_mid[BC:2 * BC, :])
                            dve.tensor_tensor(bc3[2 * BC:3 * BC, :], bc_f[2 * BC:3 * BC, :], bc_mid[2 * BC:3 * BC, :],
                                              ALU.subtract)
                            dve.drain()
                            dve.sem_inc(bc3_ready, 1)
                        if at == DTPROJ + 1:
                            dve.wait_ge(front_full, st.front(DTPROJ, q) + 1)
                            for h in range(HALVES):
                                ins = dve.tensor_scalar(z[:, h, :], front[:, h * SEQ:(h + 1) * SEQ],
                                                        dtb_sb[:, h:h + 1], None, ALU.add)
                            ins.then_inc(front_read, 1)
                            dve.drain()
                            dve.scalar_tensor_tensor(zneg[:, :, :], z[:, :, :], -1.0, z[:, :, :], ALU.mult,
                                                     ALU.min).then_inc(sp_arg, 1)
                            dve.wait_ge(sp_act, 2 * m + 1)
                            dve.tensor_scalar(ez1[:, :, :], ez[:, :, :], 1.0, None, ALU.add).then_inc(sp_arg, 1)
                            dve.drain()
                            dve.scalar_tensor_tensor(ez[:, :, :], ez1[:, :, :], -1.0, ez[:, :, :], ALU.add, ALU.subtract)
                            dve.drain()
                            dve.wait_ge(sp_act, 2 * m + 2)
                            dve.tensor_tensor(lnz[:, :, :], lnz[:, :, :], ez[:, :, :], ALU.subtract)
                            dve.drain()
                            if some(m):
                                dve.wait_ge(dA_ready, m * UNITS)
                            dve.scalar_tensor_tensor(delta[:, :, :], z[:, :, :], 0.0, lnz[:, :, :], ALU.max,
                                                     ALU.add).then_inc(delta_ready, 1)
                            dve.drain()
                            dve.tensor_tensor(udx[:, :, :], delta[:, :, :], xi[:, q, :, :], ALU.mult)
                            dve.drain()
                        k = unit(at)
                        if k is not None:
                            shape = [P, 2, HALVES, SEQ]
                            u = m * UNITS + k
                            dve.wait_ge(b_full, st.b_bank(at, q) + 1)
                            if some(last_user(u, k, NDBU)):
                                dve.wait_ge(scan_done, last_user(u, k, NDBU))
                            dve.tensor_tensor(dBu[:, k % NDBU], udx[:, :, :].unsqueeze(1).broadcast_to(shape),
                                              bP[:, :, :].unsqueeze(2).broadcast_to(shape), ALU.mult).then_inc(b_read, 1)
                        k = unit(at - SCAN_LAG)
                        if k is not None:
                            u = m * UNITS + k
                            dve.wait_ge(b_read, st.b_bank(at - SCAN_LAG, q) + 1)
                            dve.wait_ge(dA_ready, u + 1)
                            if some(last_user(u, k, NSTATE)):
                                dve.wait_ge(prod_ready, last_user(u, k, NSTATE))
                            dve.tensor_tensor_scan(state[:, k % NSTATE].rearrange("p n h t -> p (n h t)"),
                                                   dA[:, k % NDA].rearrange("p n h t -> p (n h t)"),
                                                   dBu[:, k % NDBU].rearrange("p n h t -> p (n h t)"),
                                                   0.0, ALU.mult, ALU.add).then_inc(scan_done, 1)
                        k = unit(at - SUM_LAG)
                        if k is not None:
                            u = m * UNITS + k
                            dve.wait_ge(prod_added, u + 1)
                            if some(u):
                                dve.wait_ge(sum_done, u)
                            if k == 0:
                                if some(m):
                                    dve.wait_ge(y_ready, m)
                                for h in range(HALVES):
                                    ins = dve.scalar_tensor_tensor(ysum[:, h, :], xi[:, q, h, :], d_sb[:, h:h + 1],
                                                                   prod[:, k % NPROD, 0, h], ALU.mult, ALU.add)
                            else:
                                ins = dve.tensor_tensor(ysum[:, :, :], ysum[:, :, :], prod[:, k % NPROD, 0], ALU.add)
                            ins.then_inc(sum_done, 1)
                        if at == YFIN:
                            dve.wait_ge(sum_done, (m + 1) * UNITS)
                            dve.tensor_tensor(yT[:, :, :], ysum[:, :, :], sres[:, q], ALU.mult).then_inc(y_ready, 1)
                        if at == OUTP + 1:
                            dve.wait_ge(front_full, st.front(OUTP, q) + 1)
                            dve.tensor_tensor(xs, xs, front[:, 0:SEQ_TILES * C].rearrange("p (t c) -> p t c", c=C),
                                              ALU.add).then_inc(front_read, 1)
                            dve.drain()
                    for n, (at, kind, ahead) in enumerate(st.norms):
                        t0 = (st.j + ahead) * PAIR_TILES
                        if slot == at:
                            mean_and_var(route_moments if kind == "route" else seq_moments, t0)
                        if slot == at + NORM_LAG[kind]:
                            (normalise if kind == "route" else normalise_seqs)(t0, st.norms_before + n)
                    if isinstance(st.j, int) and st.j == 0 and slot == WEIGHTS_SLOT:
                        ssm_weights()
            iterations(dve, body)

        @block.tensor
        def _(pe):
            pe.wait_ge(ident_ready, 3)

            def transpose_rows(r, use):
                pe.wait_ge(route_rows_ready, r + 1)
                if some(use):
                    pe.wait_ge(front_read, use)
                for t in range(PAIR_TILES):
                    ins = pe.transpose(front[:, t * P:(t + 1) * P], route_rows[:, t, :], ident[:, :])
                ins.then_inc(front_full, 1)

            def router_logits(r, use):
                pe.wait_ge(front_read, use)
                pe.wait_ge(lnT_ready, r + 1)
                for t in range(PAIR_TILES):
                    ins = pe.matmul(front[:, t * E:(t + 1) * E], lnT[:, t * P:(t + 1) * P], gate_sb[:, :],
                                    start=True, stop=True)
                ins.then_inc(front_full, 1)

            transpose_rows(0, 0)
            pe.wait_ge(gate_in, 16)
            router_logits(0, 1)

            def body(st):
                if isinstance(st.j, int) and st.j == 1:
                    pe.wait_ge(ssm_weights_ready, 1)
                for slot in range(st.slots):
                    if slot in st.l1:
                        i = st.l1[slot]
                        s, e = st.steps[i]
                        f = st.ffn_before + i
                        first_use = isinstance(st.j, int) and st.j == 0
                        if first_use and e % W_CHUNK == 0:
                            pe.wait_ge(w1_split, e // W_CHUNK + 1)
                        if e == 0:
                            pe.wait_ge(lnT_ready, st.routes_before + s)
                        for g in range(2):
                            if some(2 * f + g - 1):
                                pe.wait_ge(gelu_done, 2 * f + g - 1)
                            for k in range(2):
                                c0 = (2 * g + k) * P
                                pe.matmul(hP[:, g, k, :], w1_hi[:, e, c0:c0 + P], lnT_hi[s][:, :], start=True, stop=False)
                                pe.matmul(hP[:, g, k, :], w1_hi[:, e, c0:c0 + P], lnT_lo[s][:, :], start=False, stop=False)
                                ins = pe.matmul(hP[:, g, k, :], w1_lo[:, e, c0:c0 + P], lnT_hi[s][:, :], start=False, stop=True)
                            ins.then_inc(h_full, 1)
                    if slot in st.l2:
                        i = st.l2[slot]
                        s, e = st.steps[i]
                        f = st.ffn_before + i
                        if isinstance(st.j, int) and st.j == 0 and e % W_CHUNK == 0:
                            pe.wait_ge(w2_in[e // W_CHUNK], 16)
                        pe.wait_ge(gelu_done, 2 * f + 2)
                        if some(f - 1):
                            pe.wait_ge(combined, f - 1)
                        for t in range(PAIR_TILES):
                            for k in range(KF):
                                ins = pe.matmul(oP[:, i % 2, t, :], hT[:, i % 2, k, t * P:(t + 1) * P], w2_sb[:, e, k, :],
                                                start=k == 0, stop=k == KF - 1)
                        ins.then_inc(o_full, 1)
                    for r, (_, at, _, _, _) in enumerate(st.routes):
                        if slot == at:
                            transpose_rows(st.routes_before + r, st.front("rows", r))
                    for q, at in st.seq_tasks(slot):
                        m = st.seqs_before + q
                        if at in FRONT_PLACES:
                            before = st.front(at, q)
                            k = unit(at)
                            if k is not None:
                                u = m * UNITS + k
                                if k == 0:
                                    pe.wait_ge(bc3_ready, m + 1)
                                pe.wait_ge(b_read, st.b_bank(at, q))
                                for n in range(2):
                                    ins = pe.matmul(bP[:, n, :], pick[:, 2 * k + n, :], bc3[:, :],
                                                    start=True, stop=True)
                                ins.then_inc(b_full, 1)
                            if some(before):
                                pe.wait_ge(front_read, before)
                            if at == TRANSPOSE:
                                pe.wait_ge(seq_rows_ready, st.j)
                                for t in range(SEQ_TILES):
                                    ins = pe.transpose(front[:, t * P:(t + 1) * P], seq_rows[:, q * SEQ_TILES + t, :], ident[:, :])
                            elif at == CONV:
                                for h in range(HALVES):
                                    for k in range(TAPS):
                                        ins = pe.matmul(front[:, h * SEQ:(h + 1) * SEQ], convw_sb[:, k, h * P:(h + 1) * P],
                                                        xnT[:, k:k + SEQ], start=k == 0, stop=k == TAPS - 1)
                            elif at == XPROJ:
                                for h in range(HALVES):
                                    ins = pe.matmul(front[0:RANK, 0:SEQ], xproj_sb[:, h, 0:RANK], xi[:, q, h, :],
                                                    start=h == 0, stop=h == HALVES - 1)
                                for h in range(HALVES):
                                    ins = pe.matmul(front[0:3 * BC, SEQ:2 * SEQ],
                                                    xbc_sb[:, h].rearrange("p r n -> p (r n)"), xi[:, q, h, :],
                                                    start=h == 0, stop=h == HALVES - 1)
                            elif at == DTPROJ:
                                for h in range(HALVES):
                                    ins = pe.matmul(front[:, h * SEQ:(h + 1) * SEQ], dtproj_sb[:, h * P:(h + 1) * P],
                                                    rank_sb[:, :], start=True, stop=True)
                            elif at == OUTP:
                                pe.wait_ge(y_ready, m + 1)
                                for t in range(SEQ_TILES):
                                    for h in range(HALVES):
                                        ins = pe.matmul(front[:, t * C:(t + 1) * C], yT[:, h, t * P:(t + 1) * P],
                                                        outproj_sb[:, h, :], start=h == 0, stop=h == HALVES - 1)
                            else:
                                for n in range(2):
                                    ins = pe.matmul(front[:, n * SEQ:(n + 1) * SEQ], pick[:, NST + 2 * k + n, :],
                                                    bc3[:, :], start=True, stop=True)
                            ins.then_inc(front_full, 1)
                            if at == CONV:
                                if some(st.b_bank(at, q)):
                                    pe.wait_ge(b_read, st.b_bank(at, q))
                                for h in range(HALVES):
                                    ins = pe.matmul(bP[:, h, :], resw_sb[:, h * P:(h + 1) * P], xnT[:, TAPS - 1:],
                                                    start=True, stop=True)
                                ins.then_inc(b_full, 1)
                    for r, (_, at, _, _, _) in enumerate(st.routes):
                        if slot == at + 3:
                            router_logits(st.routes_before + r, st.front("logits", r))
            iterations(pe, body)


_INS = ["L0_attn_x", "L0_attn_in_proj_w", "L0_attn_conv_w", "L0_attn_conv_b", "L0_attn_x_proj_w",
        "L0_attn_dt_proj_w", "L0_attn_dt_proj_b", "L0_attn_A_log", "L0_attn_D", "L0_attn_out_proj_w",
        "L0_attn_norm_w", "L0_ffn_gate_w", "L0_ffn_w1", "L0_ffn_w2"]


def kernel(**inputs):
    import numpy as _np
    import concourse.bacc as _bacc
    from concourse import mybir as _mybir
    from concourse.bass_utils import run_bass_kernel_spmd as _run

    nc = _bacc.Bacc("TRN2", target_bir_lowering=False, num_devices=1)
    arrays, args = {}, []
    for name in _INS:
        a = _np.ascontiguousarray(inputs[name])
        arrays[f"in_{name}"] = a
        args.append(nc.dram_tensor(f"in_{name}", a.shape, _mybir.dt.from_np(a.dtype), kind="ExternalInput").ap())
    out = nc.dram_tensor("out", (BATCH, SEQ, C), F32, kind="ExternalOutput").ap()
    macaron_mamba_moe(nc, *args, out)
    r = _run(nc, [arrays], core_ids=[0])
    return r.results[0]["out"]
```
